# Optimizing a Trainium2 kernel written in Bass

```python
import numpy as np
import jax
import jax.numpy as jnp

def _softmax(x, axis=-1):
    return jax.nn.softmax(x, axis=axis)

def _gelu(x):
    return jax.nn.gelu(x, approximate=True)

def _silu(x):
    return jax.nn.silu(x)

def _sigmoid(x):
    return jax.nn.sigmoid(x)

def _layernorm(x, axis=-1, eps=1e-05):
    m = jnp.mean(x, axis=axis, keepdims=True)
    v = jnp.var(x, axis=axis, keepdims=True)
    return (x - m) / jnp.sqrt(v + eps)

def _scatter_add(tgt, idx, src, axis=0):
    return tgt.at[idx].add(src)

def _segment_sum(src, seg, n):
    return jax.ops.segment_sum(src, seg, n)
kernel_name = 'mk_gnn_preln_d4_gnn_r8_2ec0d3'

def setup_inputs(seed: int=0):
    np.random.seed(seed)
    _w = jnp.asarray

    def _rec_inputs():
        import jax
        import jax.numpy as jnp
        _gk = jax.random.key(seed)
        x = -0.0005889 + 1 * jax.random.normal(jax.random.fold_in(_gk, 1), (6250, 128), jnp.float32)
        src = jax.random.randint(jax.random.fold_in(_gk, 2), (100000,), 0, 6250, jnp.int32)
        dst = jnp.minimum((6250 * jax.random.uniform(jax.random.fold_in(_gk, 3), (100000,)) ** 2.0).astype(jnp.int32), 49999)
        _o = jnp.argsort(dst, stable=True)
        src = src[_o]
        dst = dst[_o]
        edge_attr_64 = -6.8511e-05 + 1.00004 * jax.random.normal(jax.random.fold_in(_gk, 13), (100000, 64), jnp.float32)
        edge_type_16 = jax.random.randint(jax.random.fold_in(_gk, 15), (100000,), 0, 16, jnp.int32)
        edge_weight = jax.random.uniform(jax.random.fold_in(_gk, 16), (100000,), jnp.float32, 0.0, 0.999998)
        return (x, src, dst, edge_attr_64, edge_type_16, edge_weight)
    x, src, dst, edge_attr_64, edge_type_16, edge_weight = _rec_inputs()

    def _L0_gnn_setup():
        import jax, jax.numpy as jnp
        import numpy as np
        N, E = (6250, 200000)
        F_X, F_E, F_U, H = (128, 64, 32, 128)
        B = 8
        key = jax.random.key(seed)
        ks = jax.random.split(key, 16)

        def lin(k, fan_in, fan_out):
            k1, k2 = jax.random.split(k)
            bound = 1.0 / np.sqrt(fan_in)
            W = jax.random.uniform(k1, (fan_in, fan_out), minval=-bound, maxval=bound, dtype=jnp.float32)
            b = jax.random.uniform(k2, (fan_out,), minval=-bound, maxval=bound, dtype=jnp.float32)
            return (W, b)
        W1a, b1a = lin(ks[0], F_X + F_E, H)
        W1b, b1b = lin(ks[1], H, H)
        W2a, b2a = lin(ks[2], H + F_X, H)
        W2b, b2b = lin(ks[3], H, F_X)
        return {'x': jax.random.normal(ks[4], (N, F_X), dtype=jnp.float32), 'edge_index': jax.random.randint(ks[5], (2, E), 0, N, dtype=jnp.int64), 'edge_attr': jax.random.normal(ks[6], (E, F_E), dtype=jnp.float32), 'u': jax.random.normal(ks[7], (B, F_U), dtype=jnp.float32), 'batch': jax.random.randint(ks[8], (N,), 0, B, dtype=jnp.int64), 'W1a': W1a, 'b1a': b1a, 'W1b': W1b, 'b1b': b1b, 'W2a': W2a, 'b2a': b2a, 'W2b': W2b, 'b2b': b2b}
    _L0_gnn_all = _L0_gnn_setup()
    _L0_gnn_in = {k: v for k, v in _L0_gnn_all.items() if k in ('u', 'W1a', 'b1a', 'W1b', 'b1b', 'W2a', 'b2a', 'W2b', 'b2b')}
    del _L0_gnn_all

    def _L1_gnn_setup():
        import jax, jax.numpy as jnp
        import numpy as np
        N, E, D, R, H, L = (3750, 60000, 128, 16, 4, 3)
        DH = D // H
        key = jax.random.key(seed)
        ks = jax.random.split(key, 16)
        s = 1.0 / np.sqrt(D)
        return {'feat': jax.random.normal(ks[0], (N, D), jnp.float32), 'src': jax.random.randint(ks[1], (E,), 0, N, jnp.int32), 'dst': jax.random.randint(ks[2], (E,), 0, N, jnp.int32), 'etype': jax.random.randint(ks[3], (E,), 0, R, jnp.int32), 'temporal_weight': jax.random.uniform(ks[4], (E,), jnp.float32), 'W_rel': jax.random.normal(ks[5], (L, R, D, D), jnp.float32) * s, 'b_rel': jnp.zeros((L, D), jnp.float32), 'W_loop': jax.random.normal(ks[6], (L, D, D), jnp.float32) * s, 'W_gat': jax.random.normal(ks[7], (L, D, D), jnp.float32) * s, 'attn_l': jax.random.normal(ks[8], (L, H, DH), jnp.float32) * s, 'attn_r': jax.random.normal(ks[9], (L, H, DH), jnp.float32) * s, 'b_gat': jnp.zeros((L, D), jnp.float32), 'W_fuse': jax.random.normal(ks[10], (2 * D, D), jnp.float32) * (1.0 / np.sqrt(2 * D)), 'b_fuse': jnp.zeros((D,), jnp.float32), 'W_gate': jax.random.normal(ks[11], (D + 1, D), jnp.float32) * s, 'b_gate': jnp.zeros((D,), jnp.float32)}
    _L1_gnn_all = _L1_gnn_setup()
    _L1_gnn_in = {k: v for k, v in _L1_gnn_all.items() if k in ('W_rel', 'b_rel', 'W_loop', 'W_gat', 'attn_l', 'attn_r', 'b_gat', 'W_fuse', 'b_fuse', 'W_gate', 'b_gate')}
    del _L1_gnn_all

    def _L2_gnn_setup():
        import jax, jax.numpy as jnp
        import numpy as np
        N, E, D = (12500, 75000, 128)
        BN_EPS = 1e-05
        key = jax.random.key(seed)
        ks = jax.random.split(key, 8)
        x = jax.random.normal(ks[0], (N, D), dtype=jnp.float32)
        edge_index = jax.random.randint(ks[1], (2, E), 0, N, dtype=jnp.int64)
        eps = jnp.zeros((), dtype=jnp.float32)
        s = 1.0 / np.sqrt(D)
        W1 = jax.random.uniform(ks[2], (D, D), jnp.float32, -s, s)
        b1 = jax.random.uniform(ks[3], (D,), jnp.float32, -s, s)
        gamma = jnp.ones((D,), jnp.float32)
        beta = jnp.zeros((D,), jnp.float32)
        W2 = jax.random.uniform(ks[4], (D, D), jnp.float32, -s, s)
        b2 = jax.random.uniform(ks[5], (D,), jnp.float32, -s, s)
        return {'x': x, 'edge_index': edge_index, 'eps': eps, 'W1': W1, 'b1': b1, 'gamma': gamma, 'beta': beta, 'W2': W2, 'b2': b2}
    _L2_gnn_all = _L2_gnn_setup()
    _L2_gnn_in = {k: v for k, v in _L2_gnn_all.items() if k in ('eps', 'W1', 'b1', 'gamma', 'beta', 'W2', 'b2')}
    del _L2_gnn_all

    def _L3_gnn_setup():
        import jax, jax.numpy as jnp
        import numpy as np
        N_NODES = 12500
        N_EDGES = 200000
        IN_FEATS = 128
        OUT_FEATS = 128
        K = 4
        key = jax.random.key(seed)
        k1, k2, k3, k4, k5 = jax.random.split(key, 5)
        feat = jax.random.normal(k1, (N_NODES, IN_FEATS), dtype=jnp.float32)
        src = jax.random.randint(k2, (N_EDGES,), 0, N_NODES, dtype=jnp.int32)
        dst = jax.random.randint(k3, (N_EDGES,), 0, N_NODES, dtype=jnp.int32)
        lambda_max = jnp.full((1,), 2.0, dtype=jnp.float32)
        W = jax.random.normal(k4, (K * IN_FEATS, OUT_FEATS), dtype=jnp.float32) * (1.0 / np.sqrt(K * IN_FEATS))
        b = jnp.zeros((OUT_FEATS,), dtype=jnp.float32)
        return {'feat': feat, 'src': src, 'dst': dst, 'lambda_max': lambda_max, 'W': W, 'b': b}
    _L3_gnn_all = _L3_gnn_setup()
    _L3_gnn_in = {k: v for k, v in _L3_gnn_all.items() if k in ('lambda_max', 'W', 'b')}
    del _L3_gnn_all
    return {'x': x, 'src': src, 'dst': dst, 'edge_attr_64': edge_attr_64, 'edge_type_16': edge_type_16, 'edge_weight': edge_weight, 'L0_gnn_u': _L0_gnn_in['u'], 'L0_gnn_W1a': _L0_gnn_in['W1a'], 'L0_gnn_b1a': _L0_gnn_in['b1a'], 'L0_gnn_W1b': _L0_gnn_in['W1b'], 'L0_gnn_b1b': _L0_gnn_in['b1b'], 'L0_gnn_W2a': _L0_gnn_in['W2a'], 'L0_gnn_b2a': _L0_gnn_in['b2a'], 'L0_gnn_W2b': _L0_gnn_in['W2b'], 'L0_gnn_b2b': _L0_gnn_in['b2b'], 'L1_gnn_W_rel': _L1_gnn_in['W_rel'], 'L1_gnn_b_rel': _L1_gnn_in['b_rel'], 'L1_gnn_W_loop': _L1_gnn_in['W_loop'], 'L1_gnn_W_gat': _L1_gnn_in['W_gat'], 'L1_gnn_attn_l': _L1_gnn_in['attn_l'], 'L1_gnn_attn_r': _L1_gnn_in['attn_r'], 'L1_gnn_b_gat': _L1_gnn_in['b_gat'], 'L1_gnn_W_fuse': _L1_gnn_in['W_fuse'], 'L1_gnn_b_fuse': _L1_gnn_in['b_fuse'], 'L1_gnn_W_gate': _L1_gnn_in['W_gate'], 'L1_gnn_b_gate': _L1_gnn_in['b_gate'], 'L2_gnn_eps': _L2_gnn_in['eps'], 'L2_gnn_W1': _L2_gnn_in['W1'], 'L2_gnn_b1': _L2_gnn_in['b1'], 'L2_gnn_gamma': _L2_gnn_in['gamma'], 'L2_gnn_beta': _L2_gnn_in['beta'], 'L2_gnn_W2': _L2_gnn_in['W2'], 'L2_gnn_b2': _L2_gnn_in['b2'], 'L3_gnn_lambda_max': _L3_gnn_in['lambda_max'], 'L3_gnn_W': _L3_gnn_in['W'], 'L3_gnn_b': _L3_gnn_in['b']}

def reference(x, src, dst, edge_attr_64, edge_type_16, edge_weight, L0_gnn_u, L0_gnn_W1a, L0_gnn_b1a, L0_gnn_W1b, L0_gnn_b1b, L0_gnn_W2a, L0_gnn_b2a, L0_gnn_W2b, L0_gnn_b2b, L1_gnn_W_rel, L1_gnn_b_rel, L1_gnn_W_loop, L1_gnn_W_gat, L1_gnn_attn_l, L1_gnn_attn_r, L1_gnn_b_gat, L1_gnn_W_fuse, L1_gnn_b_fuse, L1_gnn_W_gate, L1_gnn_b_gate, L2_gnn_eps, L2_gnn_W1, L2_gnn_b1, L2_gnn_gamma, L2_gnn_beta, L2_gnn_W2, L2_gnn_b2, L3_gnn_lambda_max, L3_gnn_W, L3_gnn_b):
    import jax
    import jax.numpy as jnp

    def _L0_gnn_ref(x, edge_index, edge_attr, u, batch, W1a, b1a, W1b, b1b, W2a, b2a, W2b, b2b):
        import jax, jax.numpy as jnp
        import numpy as np
        N, E = (6250, 200000)
        F_X, F_E, F_U, H = (128, 64, 32, 128)
        B = 8
        row, col = (edge_index[0], edge_index[1])
        h = jnp.concatenate([x[col], edge_attr], axis=1)
        h = jax.nn.relu(h @ W1a + b1a) @ W1b + b1b
        sums = jax.ops.segment_sum(h, row, num_segments=x.shape[0])
        cnt = jax.ops.segment_sum(jnp.ones((h.shape[0],), dtype=h.dtype), row, num_segments=x.shape[0])
        agg = sums / jnp.maximum(cnt, 1.0)[:, None]
        z = jnp.concatenate([x, agg], axis=1)
        return jax.nn.relu(z @ W2a + b2a) @ W2b + b2b

    def _L1_gnn_ref(feat, src, dst, etype, temporal_weight, W_rel, b_rel, W_loop, W_gat, attn_l, attn_r, b_gat, W_fuse, b_fuse, W_gate, b_gate):
        import jax, jax.numpy as jnp
        import numpy as np
        N, E, D, R, H, L = (3750, 60000, 128, 16, 4, 3)
        DH = D // H
        n = feat.shape[0]
        h = feat
        tw_mean = jnp.mean(temporal_weight)
        for l in range(L):
            ht = jnp.einsum('nd,rdo->nro', h, W_rel[l])
            msg = ht[src, etype]
            h_rel = jax.ops.segment_sum(msg, dst, num_segments=n)
            h_rel = h_rel + h @ W_loop[l] + b_rel[l]
            z = (h @ W_gat[l]).reshape(n, H, DH)
            el = jnp.sum(z * attn_l[l], axis=-1)
            er = jnp.sum(z * attn_r[l], axis=-1)
            e = jax.nn.leaky_relu(el[src] + er[dst], 0.2)
            m = jax.ops.segment_max(e, dst, num_segments=n)
            ex = jnp.exp(e - m[dst])
            denom = jax.ops.segment_sum(ex, dst, num_segments=n)
            alpha = ex / denom[dst]
            h_gat = jax.ops.segment_sum(alpha[:, :, None] * z[src], dst, num_segments=n)
            h_gat = h_gat.reshape(n, D) + b_gat[l]
            hc = jnp.concatenate([h_rel, h_gat], axis=1) @ W_fuse + b_fuse
            if l == 0:
                avg = jnp.full((n, 1), tw_mean, dtype=hc.dtype)
                gate = jax.nn.sigmoid(jnp.concatenate([hc, avg], axis=1) @ W_gate + b_gate)
                hc = hc * gate
            h = jax.nn.relu(hc)
        return h

    def _L2_gnn_ref(x, edge_index, eps, W1, b1, gamma, beta, W2, b2):
        import jax, jax.numpy as jnp
        import numpy as np
        N, E, D = (12500, 75000, 128)
        BN_EPS = 1e-05
        src, dst = (edge_index[0], edge_index[1])
        n = x.shape[0]
        agg = jax.ops.segment_sum(x[src], dst, num_segments=n)
        h = (1.0 + eps) * x + agg
        h = h @ W1.T + b1
        mean = jnp.mean(h, axis=0)
        var = jnp.mean(jnp.square(h - mean), axis=0)
        h = (h - mean) * jax.lax.rsqrt(var + BN_EPS) * gamma + beta
        h = jax.nn.relu(h)
        h = h @ W2.T + b2
        return x + jax.nn.relu(h)

    def _L3_gnn_ref(feat, src, dst, lambda_max, W, b):
        import jax, jax.numpy as jnp
        import numpy as np
        N_NODES = 12500
        N_EDGES = 200000
        IN_FEATS = 128
        OUT_FEATS = 128
        K = 4
        n = feat.shape[0]
        indeg = jax.ops.segment_sum(jnp.ones_like(dst, dtype=feat.dtype), dst, num_segments=n)
        D_invsqrt = jnp.clip(indeg, 1.0, None) ** (-0.5)
        D_invsqrt = D_invsqrt[:, None]

        def unn_laplacian(x):
            h = x * D_invsqrt
            agg = jax.ops.segment_sum(h[src], dst, num_segments=n)
            return agg * D_invsqrt
        re_norm = (2.0 / lambda_max)[0]
        X_0 = feat
        Xt = [X_0]
        if K > 1:
            h = unn_laplacian(X_0)
            X_1 = -re_norm * h + X_0 * (re_norm - 1.0)
            Xt.append(X_1)
        for _ in range(2, K):
            h = unn_laplacian(X_1)
            X_i = -2.0 * re_norm * h + X_1 * 2.0 * (re_norm - 1.0) - X_0
            Xt.append(X_i)
            X_1, X_0 = (X_i, X_1)
        Xt = jnp.concatenate(Xt, axis=1)
        out = Xt @ W + b
        return jax.nn.relu(out)
    edge_index = jnp.stack([src, dst])
    batch0 = jnp.zeros((6250,), jnp.int32)
    h = jnp.maximum(_layernorm(x, axis=-1), 0.0)
    x = x + _L0_gnn_ref(h, edge_index, edge_attr_64, L0_gnn_u, batch0, L0_gnn_W1a, L0_gnn_b1a, L0_gnn_W1b, L0_gnn_b1b, L0_gnn_W2a, L0_gnn_b2a, L0_gnn_W2b, L0_gnn_b2b)
    h = jnp.maximum(_layernorm(x, axis=-1), 0.0)
    x = x + _L1_gnn_ref(h, src, dst, edge_type_16, edge_weight, L1_gnn_W_rel, L1_gnn_b_rel, L1_gnn_W_loop, L1_gnn_W_gat, L1_gnn_attn_l, L1_gnn_attn_r, L1_gnn_b_gat, L1_gnn_W_fuse, L1_gnn_b_fuse, L1_gnn_W_gate, L1_gnn_b_gate)
    h = jnp.maximum(_layernorm(x, axis=-1), 0.0)
    x = x + _L2_gnn_ref(h, edge_index, L2_gnn_eps, L2_gnn_W1, L2_gnn_b1, L2_gnn_gamma, L2_gnn_beta, L2_gnn_W2, L2_gnn_b2)
    h = jnp.maximum(_layernorm(x, axis=-1), 0.0)
    x = x + _L3_gnn_ref(h, src, dst, L3_gnn_lambda_max, L3_gnn_W, L3_gnn_b)
    return x

_drawn_inputs = setup_inputs


def setup_inputs(seed=0):
    import zlib

    import numpy as np

    out = dict(_drawn_inputs(seed))
    spreads = {'L1_gnn_b_rel': (0.0, 0.1),
     'L1_gnn_b_gat': (0.0, 0.1),
     'L1_gnn_b_fuse': (0.0, 0.1),
     'L1_gnn_b_gate': (0.0, 0.332),
     'L2_gnn_gamma': (1.0, 0.6),
     'L2_gnn_beta': (0.0, 2.0),
     'L3_gnn_b': (0.0, 0.8)}
    factors = {'edge_attr_64': 8.0,
     'edge_weight': 64.0,
     'L0_gnn_W1a': 3.154,
     'L0_gnn_b1a': 8.0,
     'L0_gnn_W1b': 2.89,
     'L0_gnn_b1b': 5.389,
     'L0_gnn_b2a': 3.194,
     'L2_gnn_W1': 2.911,
     'L2_gnn_b1': 64.0,
     'L2_gnn_b2': 8.0}
    for name, (base, spread) in spreads.items():
        noise = np.random.default_rng([zlib.crc32(name.encode()), seed]).standard_normal(out[name].shape)
        drawn = base * np.exp(spread * noise) if base else spread * noise
        out[name] = jnp.asarray(drawn.astype(out[name].dtype))
    for name, factor in factors.items():
        out[name] = (out[name] * factor).astype(out[name].dtype)
    return out
```

```python
from contextlib import ExitStack

import numpy as np
import concourse.bass as bass
from concourse import mybir

ALU = mybir.AluOpType
ACT = mybir.ActivationFunctionType
F32 = mybir.dt.float32
BF16 = mybir.dt.bfloat16
I32 = mybir.dt.int32
AX = mybir.AxisListType

P = 128
D = 128
N = 6250
E = 100000
FE = 64
R = 16
H = 4
DH = D // H
NQ = -(-N // (4 * P))
NW = 4 * NQ
NPAD = NW * P
G = 2
BODY = 12
GROUPS = 6
VALS = 3
TG = 2 * G
BMAX = (E + NW * G * P) // (G * P)
NB = -(-BMAX // BODY) * BODY
ITERS = NB // BODY
T = NB * G
EC = 784
LASTC = E - (P - 1) * EC
CH = 8
PITCH = 936
FILL = 36
K0 = FE + 2
K1 = 4
assert PITCH >= T + TG * GROUPS and (P * EC - E) <= (PITCH - T) * P and PITCH % FILL == 0
assert GROUPS % VALS == 0
assert EC % (2 * CH) == 0 and LASTC % (2 * CH) == 0
FZ = D + H
KT = D + 3 * H // 2
ARENA = 23600
NCONST = 9 + 11 + 16
BIG = 1e30
NGR = ITERS * GROUPS
LAYERS = 3


class Chain:

    def __init__(self, sem):
        self.sem, self.n = sem, 0

    def link(self, eng, ins):
        ins.then_inc(self.sem, 1)
        self.n = self.n + 1
        eng.wait_ge(self.sem, self.n)


class Rounds(Chain):

    def __init__(self, sem, per):
        super().__init__(sem)
        self.per, self.k, self.rnd = per, 0, 0

    def begin(self, rnd):
        self.rnd, self.k = rnd, 0

    def link(self, eng, ins):
        ins.then_inc(self.sem, 1)
        self.k += 1
        eng.wait_ge(self.sem, self.rnd * self.per + self.k)

    def end(self):
        assert self.k == self.per, (self.k, self.per)


class Steps:

    def __init__(self, sem, *names):
        self.sem, self.names = sem, names

    def after(self, rnd, name):
        return rnd * len(self.names) + self.names.index(name) + 1


def build(nc, a, out):
    with ExitStack() as ctx:
        def sb(name, shape, dt=F32):
            return ctx.enter_context(nc.sbuf_tensor(name, shape, dt))

        def sem(name):
            return ctx.enter_context(nc.semaphore(name))

        def dram(name, shape, dt=F32):
            return nc.dram_tensor(name, shape, dt, kind="Internal").ap()

        arena = sb("arena", [P, ARENA])
        cut = [0]

        def carve(shape, dt=F32):
            words = int(np.prod(shape)) // (2 if dt == BF16 else 1)
            v = arena[:, cut[0]:cut[0] + words]
            cut[0] += words
            assert cut[0] <= ARENA, cut
            if dt != F32:
                v = v.bitcast(dt)
            if len(shape) > 1:
                names = "abcd"[:len(shape)]
                v = v.rearrange(f"p ({' '.join(names)}) -> p {' '.join(names)}", **dict(zip(names, shape)))
            return v

        x_pad = dram("x_pad", [NPAD, D])
        h0_d = dram("h0_d", [NPAD, D])
        y_d = dram("y_d", [NPAD, D])
        x1_d = dram("x1_d", [NPAD, D])
        hT_d = dram("hT_d", [P, NPAD])
        rec0_d = dram("rec0_d", [P * PITCH, K0], I32)
        rec1_d = dram("rec1_d", [P * PITCH, K1], I32)
        histz_d = dram("histz_d", [NB * P, FZ])
        hista_d = dram("hista_d", [NB * P, FZ])
        tab_d = dram("tab_d", [NPAD * R, KT])
        z_d = dram("z_d", [NPAD, FZ])
        er_d = dram("er_d", [NPAD, H])
        x2_d = dram("x2_d", [NPAD, D])
        h2_d = dram("h2_d", [NPAD, D])
        x3_d = dram("x3_d", [NPAD, D])
        cheb_d = dram("cheb_d", [5 * NPAD, D])
        chtab_d = dram("chtab_d", [NPAD, D])
        acc_d = dram("acc_d", [NPAD, D])

        iota_i = sb("iota_i", [P, NB], I32)
        pidx_i = sb("pidx_i", [P, 1], I32)
        iota = sb("iota", [P, NB])
        pidx = sb("pidx", [P, 1])
        ident = sb("ident", [P, P])
        tri = sb("tri", [P, P])
        ones = sb("ones", [P, P])
        zeros = sb("zeros", [P, 7 * D])
        eps_ln = sb("eps_ln", [P, 1])
        w1a_x = sb("w1a_x", [P, D])
        w1a_e = sb("w1a_e", [FE, D])
        w1b = sb("w1b", [P, D])
        w2a = sb("w2a", [P, 2, D])
        w2b = sb("w2b", [P, D])
        b1a_r = sb("b1a_r", [P, D])
        b1b_r = sb("b1b_r", [P, D])
        b2b_r = sb("b2b_r", [P, D])
        b2a_c = sb("b2a_c", [P, 1])
        src_i = carve([EC], I32)
        dst_i = carve([EC], I32)
        ety_i = carve([EC], I32)
        win_i = carve([EC], I32)
        low_i = carve([EC], I32)
        win_f = carve([EC], F32)
        mask_i = carve([EC], I32)
        scan_f = carve([EC], F32)
        slot_f = carve([EC], F32)
        spare_i = carve([EC], I32)
        addr = [carve([EC], I32) for r in range(2)]
        field0 = carve([EC, 2], I32)
        field1 = carve([EC, K1], I32)
        count = sb("count", [P, NW])
        nblk_i = sb("nblk_i", [P, NW], I32)
        nblk = sb("nblk", [P, NW])
        bend = sb("bend", [P, NW])
        bstart = sb("bstart", [P, NW])
        base = sb("base", [P, NW])
        last_i = [sb(f"last_i{r}", [P, NW], I32) for r in range(2)]
        wofb = [sb(f"wofb{r}", [P, NB]) for r in range(2)]
        keep = [sb(f"keep{r}", [P, NB]) for r in range(2)]
        fill0 = carve([FILL, K0], I32)
        fill1 = carve([FILL, K1], I32)
        pay0 = carve([2, CH, K0], I32)
        pay1 = carve([2, CH, K1], I32)
        payaddr = carve([2, CH], I32)
        rec0 = carve([GROUPS, TG, K0], I32)
        hpre = carve([VALS, TG, D])
        hid = carve([VALS, TG, D + 1])
        rec1 = sb("rec1", [P, GROUPS, TG, K1], I32)
        rows = sb("rows", [P, GROUPS, TG, D + 1])
        onehot = sb("onehot", [P, GROUPS, TG, P])
        eaT = sb("eaT", [FE, TG, P])
        run = sb("run", [P, BODY, FZ])
        cut[0] = 0
        wrel = carve([R, D])
        rows1 = carve([GROUPS, TG, KT])
        zrow = carve([GROUPS, TG, FZ])
        pen = carve([GROUPS, TG, P], BF16)
        bmax = carve([NB, H])
        wmax = carve([NB, H])
        rest = arena[:, cut[0] - 2 * NB * H:cut[0]].rearrange("p (b c) -> p b c", b=NB)
        stage_at = cut[0]
        tabq = [carve([R, KT]) for _ in range(2)]
        cut[0] = stage_at
        erm = carve([NB, 2 * H])
        erm3 = carve([NB, 3 * 2 * H], BF16)
        cut[0] = stage_at
        uT = carve([NPAD])
        identb = sb("identb", [P, P], BF16)
        code = sb("code", [3 * H, H])
        sel = sb("sel", [3 * H, H, P], BF16)
        elT = sb("elT", [3 * H, TG, P], BF16)
        ohT = sb("ohT", [P, TG, P], BF16)
        erme = sb("erme", [P, TG, 2 * H])
        att = sb("att", [P, TG, H])
        zex = sb("zex", [P, VALS, TG, FZ])
        hmask = sb("hmask", [P, H])
        pidx5 = sb("pidx5", [P, 1], I32)
        acol = sb("acol", [P, 2])
        amat = sb("amat", [P, 2 * H])
        wgat = sb("wgat", [P, D + 2 * H])
        wgatT = sb("wgatT", [P, P])
        wloop = sb("wloop", [P, D])
        wfuse = sb("wfuse", [P, 2, D])
        wgate = sb("wgate", [P, D])
        brel_c = sb("brel_c", [P, 1])
        bgat_c = sb("bgat_c", [P, 1])
        bfuse_c = sb("bfuse_c", [P, 1])
        bgate_c = sb("bgate_c", [P, 1])
        wg_last = sb("wg_last", [P, 1])
        gbias_c = sb("gbias_c", [P, 1])
        gsel = sb("gsel", [P, 2, 3])
        ew = sb("ew", [P, E // 125])
        ewsum = sb("ewsum", [P, 1])
        zq = sb("zq", [P, 4, FZ + H])
        el3 = sb("el3", [P, 4, 3 * H], BF16)
        elr = sb("elr", [P, 4, H])
        kpen = sb("kpen", [P, NB])
        erw = sb("erw", [NW, P, H])
        woh = sb("woh", [NW, NB])
        den = sb("den", [P, 4, H])
        w1T = sb("w1T", [P, P])
        w2T = sb("w2T", [P, P])
        w12 = sb("w12", [P, 2, P])
        b1_c = sb("b1_c", [P, 1])
        b2_r = sb("b2_r", [P, D])
        gamma_c = sb("gamma_c", [P, 1])
        beta_c = sb("beta_c", [P, 1])
        ope = sb("ope", [P, 1])
        bnst = sb("bnst", [P, NQ + 1, 6])
        bnmv = sb("bnmv", [P, 2])
        bnsd = sb("bnsd", [P, 1])
        bnr = sb("bnr", [P, 1])
        bnscale = sb("bnscale", [P, 1])
        bnshift = sb("bnshift", [P, 1])
        dinv = sb("dinv", [P, NW])
        w3 = sb("w3", [P, 4, D])
        w3k = sb("w3k", [P, D])
        b3_r = sb("b3_r", [P, D])
        lam = sb("lam", [P, 1])
        rn = sb("rn", [P, 1])
        coef = sb("coef", [P, 3, 3])
        win_sum = sb("win_sum", [P, 4, FZ])
        xq = sb("xq", [P, 4, D])
        hq = sb("hq", [P, 4, D])
        yq = sb("yq", [P, 4, D])
        aq = sb("aq", [P, 4, D])
        xo = sb("xo", [P, 4, D])
        ho = sb("ho", [P, 4, D])
        tA = sb("tA", [P, 4, D])
        tB = sb("tB", [P, 4, D])
        tC = sb("tC", [P, 4, D])
        stat = sb("stat", [P, 4, 6])
        mv = sb("mv", [P, 4, 2])
        sd = sb("sd", [P, 4])
        rstd = sb("rstd", [P, 4])
        nmr = sb("nmr", [P, 4])
        cn = sb("cn", [P, 4])
        rc = sb("rc", [P, 4])
        ind = sb("ind", [P, 4])

        tD = sb("tD", [P, 4, D])
        tE = sb("tE", [P, 4, D])

        psum = ctx.enter_context(nc.psum_tensor("psum", [P, 8, 512], F32))
        bank = [psum[:, j, :] for j in range(8)]

        def b4(j):
            return psum[:, j, :].rearrange("p (t f) -> p t f", t=4)

        const_ld = sem("const_ld")
        pool_io = sem("pool_io")
        chain = Chain(sem("dve_chain"))
        filled = sem("filled")
        fill_ready = sem("fill_ready")
        counted = sem("counted")
        prefixed = sem("prefixed")
        sorted_ = sem("sorted")
        pay_ld = [sem(f"pay_ld{s}") for s in range(2)]
        pay_rdy = sem("pay_rdy")
        scat = [sem(f"scat{s}") for s in range(2)]
        rec_ld = [sem(f"rec_ld{g}") for g in range(GROUPS)]
        gata = [sem(f"gata{g}") for g in range(GROUPS)]
        gatz = [sem(f"gatz{g}") for g in range(GROUPS)]
        gatx = [sem(f"gatx{g}") for g in range(GROUPS)]
        hist_st = [sem(f"hist_st{j}") for j in range(BODY)]
        oh_rdy = sem("oh_rdy")
        pen_rdy = sem("pen_rdy")
        summed = sem("summed")
        run_rdy = sem("run_rdy")
        attw_ready = sem("attw_ready")
        wT_ready = sem("wT_ready")
        st_tab = [sem(f"st_tab{s}") for s in range(2)]
        tw_sum = sem("tw_sum")
        tw_tot = sem("tw_tot")
        layer_ld = sem("layer_ld")
        settled = sem("settled")
        bnorm = sem("bnorm")

        ld = {n: sem(f"ld_{n}") for n in ("A0", "F0", "T1", "M", "F1", "A2", "F2", "B2", "F3", "O")}
        st = {n: sem(f"st_{n}") for n in ("A0", "F0", "T1", "F1", "A2", "B2", "F3", "O")}
        ch = {n: Rounds(sem(f"ch_{n}"), per) for n, per in
              (("A0", 2), ("F0", 6), ("T1", 5), ("M", 16), ("E1b", 4), ("F1", 4), ("A2", 3), ("B2", 5), ("F3", 3),
               ("O", 1))}

        e0pe = Steps(sem("e0pe"), "turned", "projected")
        e0act = Steps(sem("e0act"), "turned", "relu")
        e0dve = Steps(sem("e0dve"), "added")
        A0d = Steps(sem("a0d"), "stats", "ln", "y")
        A0a = Steps(sem("a0a"), "sd", "h", "hT")
        A0p = Steps(sem("a0p"), "hT", "y")
        F0d = Steps(sem("f0d"), "sm", "agg", "stats", "ln")
        F0a = Steps(sem("f0a"), "T", "agT", "u", "sd", "h", "h1T")
        F0p = Steps(sem("f0p"), "T", "agg", "agT", "u", "o", "h1T")
        T1p = Steps(sem("t1p"), "z")
        T1d = Steps(sem("t1d"), "z")
        T1tp = Steps(sem("t1tp"), "messages")
        T1td = Steps(sem("t1td"), "copied")
        T1ta = Steps(sem("t1ta"), "copied")
        E1p = Steps(sem("e1p"), "elT", "max0", "max1")
        E1a = Steps(sem("e1a"), "elT")
        E1d = Steps(sem("e1d"), "max0", "max1")
        Mp = Steps(sem("mp"), "er")
        Md = Steps(sem("md"), "erm3")
        EBp = Steps(sem("ebp"), "ohT", "erm")
        EBa = Steps(sem("eba"), "ohT", "exp")
        EBd = Steps(sem("ebd"), "logits", "weighted")
        F1d = Steps(sem("f1d"), "mean", "gate")
        F1a = Steps(sem("f1a"), "rel", "gat", "hc", "gate")
        F1p = Steps(sem("f1p"), "T", "hc", "gate")
        A2d = Steps(sem("a2d"), "stats", "ln")
        A2a = Steps(sem("a2a"), "sd", "h")
        A2p = Steps(sem("a2p"), "T")
        F2d = Steps(sem("f2d"), "cn", "pre")
        F2a = Steps(sem("f2a"), "sd", "T", "u")
        F2p = Steps(sem("f2p"), "T", "u")
        B2d = Steps(sem("b2d"), "stats", "ln", "table", "acc")
        B2a = Steps(sem("b2a"), "v", "sd", "h", "T")
        B2p = Steps(sem("b2p"), "y", "T", "acc")
        F3d = Steps(sem("f3d"), "x", "table", "acc")
        F3a = Steps(sem("f3a"), "T")
        F3p = Steps(sem("f3p"), "T", "acc")

        def settle(eng):
            eng.sem_inc(settled, 1)

        def quad_of(ap, q, base=0):
            return ap[bass.ds(base + q * 512, 512), :].rearrange("(p t) f -> p t f", t=4)

        const_total = 16 * NCONST
        block = ctx.enter_context(nc.Block())

        @block.sync
        def _(sp):
            n = [0]

            def const(dst, src):
                sp.dma_start(dst, src).then_inc(const_ld, 16)
                n[0] += 16

            def col(ap):
                return ap.rearrange("(k c) -> k c", c=1)

            def edges(dst, src):
                const(dst[0:112, :], src[0:112 * EC].rearrange("(p c) -> p c", c=EC))
                const(dst[112:127, :], src[112 * EC:127 * EC].rearrange("(p c) -> p c", c=EC))
                const(dst[127:128, 0:LASTC], src[127 * EC:E].rearrange("(p c) -> p c", p=1))

            sp.wait_ge(fill_ready, 1)
            edges(src_i, a["src"])
            edges(dst_i, a["dst"])
            edges(ety_i, a["edge_type_16"])
            const(w1a_x[:, :], a["L0_gnn_W1a"][0:D, :])
            const(w1a_e[:, :], a["L0_gnn_W1a"][D:D + FE, :])
            const(w1b[:, :], a["L0_gnn_W1b"])
            const(w2a[:, :, :], a["L0_gnn_W2a"].rearrange("(c k) f -> k c f", k=P))
            const(w2b[:, :], a["L0_gnn_W2b"])
            const(b1a_r[:, :], a["L0_gnn_b1a"].partition_broadcast(P))
            const(b1b_r[:, :], a["L0_gnn_b1b"].partition_broadcast(P))
            const(b2b_r[:, :], a["L0_gnn_b2b"].partition_broadcast(P))
            const(b2a_c[:, :], col(a["L0_gnn_b2a"]))
            const(wfuse[:, :, :], a["L1_gnn_W_fuse"].rearrange("(c k) f -> k c f", k=P))
            const(wgate[:, :], a["L1_gnn_W_gate"][0:D, :])
            const(bfuse_c[:, :], col(a["L1_gnn_b_fuse"]))
            const(bgate_c[:, :], col(a["L1_gnn_b_gate"]))
            const(wg_last[:, :], a["L1_gnn_W_gate"][D:D + 1, :].rearrange("c k -> k c"))
            const(ew[0:125, :], a["edge_weight"].rearrange("(p c) -> p c", p=125))
            const(w12[:, 0, :], a["L2_gnn_W1"])
            const(w12[:, 1, :], a["L2_gnn_W2"])
            const(b1_c[:, :], col(a["L2_gnn_b1"]))
            const(b2_r[:, :], a["L2_gnn_b2"].partition_broadcast(P))
            const(gamma_c[:, :], col(a["L2_gnn_gamma"]))
            const(beta_c[:, :], col(a["L2_gnn_beta"]))
            const(ope[:, :], a["L2_gnn_eps"].partition_broadcast(P))
            const(w3[:, :, :], a["L3_gnn_W"].rearrange("(c k) f -> k c f", k=P))
            const(b3_r[:, :], a["L3_gnn_b"].partition_broadcast(P))
            const(lam[:, :], a["L3_gnn_lambda_max"].partition_broadcast(P))
            const(x_pad[0:N, :], a["x"])
            sp.wait_ge(fill_ready, 2)
            const(x_pad[N:NPAD, :].rearrange("(r m) f -> r (m f)", m=7), zeros[0:(NPAD - N) // 7, :])
            assert n[0] == const_total, n
            view0 = rec0_d.rearrange("(p c) k -> p c k", p=P)
            view1 = rec1_d.rearrange("(p c) k -> p c k", p=P)
            for k in range(PITCH // FILL):
                c = slice(k * FILL, (k + 1) * FILL)
                if k >= 2:
                    sp.dma_start(view0[:, c, :], fill0[:, :, :]).then_inc(filled, 16)
                sp.dma_start(view1[:, c, :], fill1[:, :, :]).then_inc(st_tab[k] if k < 2 else filled, 16)
            for j in range(BODY):
                sp.dma_start(histz_d[j * P:(j + 1) * P, :], run[:, j, :]).then_inc(hist_st[j], 16)
            sp.wait_ge(const_ld, const_total)

            def load(name, dst, src):
                sp.dma_start(dst, src).then_inc(ld[name], 16)

            def store(name, dst, src):
                sp.dma_start(dst, src).then_inc(st[name], 16)

            def stored(name, rnd, per):
                sp.wait_ge(st[name], (rnd * per + per) * 16)
                settle(sp)

            def feature_quad(q):
                return hT_d[:, bass.ds(q * 512, 512)].rearrange("p (t f) -> p t f", t=4)

            with sp.Fori(0, NQ) as q:
                load("A0", xq[:, :, :], quad_of(x_pad, q))
                sp.wait_ge(A0a.sem, A0a.after(q, "h"))
                store("A0", quad_of(h0_d, q), ho[:, :, :])
                sp.wait_ge(A0d.sem, A0d.after(q, "y"))
                store("A0", quad_of(y_d, q), yq[:, :, :])
                stored("A0", q, 2)

            ea = a["edge_attr_64"].bitcast(I32)

            def pay_chunks(k, s, whole):
                c = (2 * k + s) * CH
                sp.wait_ge(scat[s], 16 + 128 * k)
                for lo, hi in ((0, 112), (112, 127)) + (((127, 128),) if whole else ()):
                    if lo < 127:
                        v = ea[lo * EC:hi * EC, :].rearrange("(p c) f -> p c f", c=EC)
                    else:
                        v = ea[127 * EC:E, :].rearrange("(p c) f -> p c f", p=1)
                    sp.dma_start(pay0[lo:hi, s, :, 0:FE], v[:, bass.ds(c, CH), :]).then_inc(pay_ld[s], 16)
                if not whole:
                    sp.sem_inc(pay_ld[s], 16)

            with sp.Fori(0, LASTC // (2 * CH)) as k:
                for s in range(2):
                    pay_chunks(k, s, True)
            with sp.Fori(LASTC // (2 * CH), EC // (2 * CH)) as k:
                for s in range(2):
                    pay_chunks(k, s, False)
            for s in range(2):
                sp.wait_ge(scat[s], 16 + 128 * (EC // (2 * CH)))

            def edge_pass(view, ring, r, hist, width):
                def records(g, c):
                    sp.dma_start(ring[:, g, :, :], view[:, bass.ds(c, TG), :]).then_inc(rec_ld[g], 16)

                for g in range(GROUPS):
                    records(g, g * TG)
                with sp.Fori(0, ITERS) as i:
                    for g in range(GROUPS):
                        for b in range(2):
                            j = 2 * g + b
                            sp.wait_ge(run_rdy, (r * NB + BODY + 1) + i * BODY + j)
                            sp.dma_start(hist[bass.ds((i * BODY + j) * P, P), 0:width],
                                         run[:, j, 0:width]).then_inc(hist_st[j], 16)
                        records(g, (i + 1) * (GROUPS * TG) + g * TG)
                for g in range(GROUPS):
                    sp.wait_ge(rec_ld[g], (r + 1) * (16 * (ITERS + 1)))
                for j in range(BODY):
                    sp.wait_ge(hist_st[j], (r + 1) * (16 * ITERS) + 16)
                settle(sp)

            edge_pass(view0, rec0, 0, histz_d, D + 1)

            def window_sums(name, which, hist, width, q, dst):
                for t in range(4):
                    at = sp.value_load(last_i[which][0:1, bass.ds(q * 4 + t, 1)], min_val=0, max_val=NB - 1)
                    load(name, dst[:, t, 0:width], hist[bass.ds(at * P, P), 0:width])

            with sp.Fori(0, NQ) as q:
                window_sums("F0", 0, histz_d, D + 1, q, win_sum)
                load("F0", xq[:, :, :], quad_of(x_pad, q))
                load("F0", hq[:, :, :], quad_of(h0_d, q))
                sp.wait_ge(F0d.sem, F0d.after(q, "stats"))
                store("F0", quad_of(x1_d, q), xo[:, :, :])
                sp.wait_ge(F0a.sem, F0a.after(q, "h1T"))
                settle(sp)
                store("F0", feature_quad(q), tC[:, :, :])
                stored("F0", q, 2)
            for s in range(2):
                sp.wait_ge(scat[s], 16 + 256 * (EC // (2 * CH)))

            with sp.Fori(0, LAYERS) as l:
                one = bass.ds(l, 1)
                for dst, src in (
                    (wrel[:, 0:R // 2, :], a["L1_gnn_W_rel"][one, 0:R // 2].rearrange("a r k f -> k (a r) f")),
                    (wrel[:, R // 2:R, :], a["L1_gnn_W_rel"][one, R // 2:R].rearrange("a r k f -> k (a r) f")),
                    (wloop[:, :], a["L1_gnn_W_loop"][one].rearrange("a k f -> (a k) f")),
                    (wgat[:, 0:D], a["L1_gnn_W_gat"][one].rearrange("a k f -> (a k) f")),
                    (acol[:, 0:1], a["L1_gnn_attn_l"][one].rearrange("a h d -> (h d) a")),
                    (acol[:, 1:2], a["L1_gnn_attn_r"][one].rearrange("a h d -> (h d) a")),
                    (brel_c[:, :], a["L1_gnn_b_rel"][one].rearrange("a k -> k a")),
                    (bgat_c[:, :], a["L1_gnn_b_gat"][one].rearrange("a k -> k a")),
                ):
                    sp.dma_start(dst, src).then_inc(layer_ld, 16)
                with sp.Fori(0, NQ) as q:
                    rnd = l * NQ + q
                    load("T1", tA[:, :, :], feature_quad(q))
                    sp.wait_ge(T1d.sem, T1d.after(rnd, "z"))
                    settle(sp)
                    store("T1", er_d[bass.ds(q * 512, 512), :].rearrange("(t p) h -> p t h", p=P), zq[:, :, FZ:FZ + H])
                    store("T1", quad_of(z_d, q), zq[:, :, 0:FZ])
                    for t in range(4):
                        sp.wait_ge(T1td.sem, (rnd * 4 + t) * 2 + 4)
                        sp.wait_ge(T1ta.sem, (rnd * 4 + t) * 2 + 4)
                        sp.dma_start(tab_d[bass.ds(q * (512 * R), 512 * R), :].rearrange(
                            "(p t r) k -> p t (r k)", t=4, r=R)[:, t, :],
                            tabq[t % 2][:, :, :].rearrange("p r k -> p (r k)")).then_inc(st_tab[t % 2], 16)
                    stored("T1", rnd, 2)
                for s in range(2):
                    sp.wait_ge(st_tab[s], l * (32 * NQ) + 16 + 32 * NQ)
                edge_pass(view1, rec1, 2 * l + 1, hista_d, D)
                load("M", erw[:, :, :], er_d.rearrange("(w p) h -> w p h", p=P))
                sp.wait_ge(Md.sem, Md.after(l, "erm3"))
                settle(sp)
                edge_pass(view1, rec1, 2 * l + 2, histz_d, FZ)
                with sp.Fori(0, NQ) as q:
                    rnd = l * NQ + q
                    window_sums("F1", 1, hista_d, D, q, aq)
                    window_sums("F1", 1, histz_d, FZ, q, win_sum)
                    load("F1", tA[:, :, :], feature_quad(q))
                    sp.wait_ge(F1d.sem, F1d.after(rnd, "gate"))
                    settle(sp)
                    store("F1", feature_quad(q), xo[:, :, :])
                    stored("F1", rnd, 1)

            with sp.Fori(0, NQ) as q:
                load("A2", tA[:, :, :], feature_quad(q))
                load("A2", xq[:, :, :], quad_of(x1_d, q))
                sp.wait_ge(A2d.sem, A2d.after(q, "stats"))
                store("A2", quad_of(x2_d, q), xo[:, :, :])
                sp.wait_ge(A2a.sem, A2a.after(q, "h"))
                store("A2", quad_of(h2_d, q), ho[:, :, :])
                stored("A2", q, 2)
            edge_pass(view1, rec1, 7, histz_d, D + 1)
            with sp.Fori(0, NQ) as q:
                window_sums("F2", 1, histz_d, D + 1, q, win_sum)
                load("F2", hq[:, :, :], quad_of(h2_d, q))
                sp.wait_ge(F2a.sem, F2a.after(q, "u"))
                settle(sp)
            with sp.Fori(0, NQ) as q:
                load("B2", xq[:, :, :], quad_of(x2_d, q))
                load("B2", hq[:, :, :], quad_of(h2_d, q))
                sp.wait_ge(B2d.sem, B2d.after(q, "stats"))
                store("B2", quad_of(x3_d, q), xo[:, :, :])
                sp.wait_ge(B2a.sem, B2a.after(q, "h"))
                store("B2", quad_of(cheb_d, q), ho[:, :, :])
                store("B2", quad_of(cheb_d, q, NPAD), ho[:, :, :])
                sp.wait_ge(B2d.sem, B2d.after(q, "table"))
                store("B2", quad_of(chtab_d, q), yq[:, :, :])
                sp.wait_ge(B2d.sem, B2d.after(q, "acc"))
                store("B2", quad_of(acc_d, q), aq[:, :, :])
                stored("B2", q, 5)
            with sp.Fori(0, LAYERS) as k:
                edge_pass(view1, rec1, k + 8, histz_d, D + 1)
                with sp.Fori(0, NQ) as q:
                    rnd = k * NQ + q
                    window_sums("F3", 1, histz_d, D, q, win_sum)
                    load("F3", xq[:, :, :], quad_of(cheb_d, q, k * NPAD))
                    load("F3", hq[:, :, :], quad_of(cheb_d, q, k * NPAD + NPAD))
                    load("F3", aq[:, :, :], quad_of(acc_d, q))
                    sp.wait_ge(F3d.sem, F3d.after(rnd, "x"))
                    settle(sp)
                    store("F3", quad_of(cheb_d, q, k * NPAD + 2 * NPAD), xo[:, :, :])
                    sp.wait_ge(F3d.sem, F3d.after(rnd, "table"))
                    settle(sp)
                    store("F3", quad_of(chtab_d, q), yq[:, :, :])
                    sp.wait_ge(F3d.sem, F3d.after(rnd, "acc"))
                    settle(sp)
                    store("F3", quad_of(acc_d, q), ho[:, :, :])
                    stored("F3", rnd, 3)
            with sp.Fori(0, NQ) as q:
                load("O", xq[:, :, :], quad_of(x3_d, q))
                load("O", aq[:, :, :], quad_of(acc_d, q))
                sp.wait_ge(ch["O"].sem, q * 2 + 2)
                settle(sp)
                store("O", quad_of(x1_d, q), xo[:, :, :])
                stored("O", q, 1)
            sp.dma_start(out[:, :], x1_d[0:N, :]).then_inc(const_ld, 16)
            sp.wait_ge(const_ld, const_total + 16)

        @block.gpsimd
        def _(pool):
            nc.gpsimd.iota(iota_i[:, :], [[1, NB]], base=0, channel_multiplier=0)
            nc.gpsimd.iota(pidx_i[:, :], [[0, 1]], base=0, channel_multiplier=1)
            nc.gpsimd.iota(spare_i[:, :], [[1, EC]], base=T * P - LASTC, channel_multiplier=0).then_inc(pool_io, 1)
            pool.wait_ge(fill_ready, 2)
            for k in range(2):
                pool.dma_start(rec0_d.rearrange("(p c) k -> p c k", p=P)[:, k * FILL:(k + 1) * FILL, :],
                               fill0[:, :, :]).then_inc(scat[k], 16)
            pool.wait_ge(filled, 16 * (2 * (PITCH // FILL) - 4))
            for s in range(2):
                pool.wait_ge(st_tab[s], 16)
                pool.wait_ge(scat[s], 16)

            def scatter(r, rec, pay):
                with pool.Fori(0, EC // (2 * CH)) as k:
                    for s in range(2):
                        pool.wait_ge(pay_rdy, r * (EC // CH) + 2 * k + s + 1)
                        settle(pool)
                        for c in range(CH):
                            nc.gpsimd.indirect_dma_start(
                                out=rec, out_offset=bass.IndirectOffsetOnAxis(ap=payaddr[:, s, c:c + 1], axis=0),
                                in_=pay[:, s, c, :], in_offset=None).then_inc(scat[s], 16)

            def gather_pass(r, table, ring, col, dst, width, gat):
                with pool.Fori(0, ITERS) as i:
                    for g in range(GROUPS):
                        pool.wait_ge(rec_ld[g], r * (16 * (ITERS + 1)) + 16 + i * 16)
                        pool.wait_ge(run_rdy, r * NB + i * BODY + 2 * g + 2)
                        settle(pool)
                        for t in range(TG):
                            nc.gpsimd.indirect_dma_start(
                                out=dst[:, g, t, 0:width], out_offset=None, in_=table,
                                in_offset=bass.IndirectOffsetOnAxis(ap=ring[:, g, t, col:col + 1], axis=0)
                            ).then_inc(gat[g], 16)

            scatter(0, rec0_d, pay0)
            scatter(1, rec1_d, pay1)
            gather_pass(0, y_d, rec0, FE, rows, D, gata)
            with pool.Fori(0, LAYERS) as l:
                gather_pass(2 * l + 1, tab_d, rec1, 0, rows1, KT, gata)
                gather_pass(2 * l + 2, z_d, rec1, 1, zrow, FZ, gatz)
            gather_pass(7, h2_d, rec1, 1, rows, D, gatx)
            with pool.Fori(0, LAYERS) as k:
                gather_pass(k + 8, chtab_d, rec1, 1, rows, D, gatx)

        @block.vector
        def _(dve):
            v = nc.vector

            def link(ins):
                chain.link(dve, ins)

            def then(steps, ins, rnd, name):
                ins.then_inc(steps.sem, 1)
                dve.wait_ge(steps.sem, steps.after(rnd, name))

            def over(col_ap, n=4):
                return col_ap.unsqueeze(2).to_broadcast([P, n, D])

            def row4(r):
                return r[:, :].unsqueeze(1).to_broadcast([P, 4, D])

            v.memset(src_i[:, :], 1 << 20)
            v.memset(dst_i[:, :], 1 << 20)
            v.memset(ety_i[:, :], 0).then_inc(fill_ready, 1)
            link(v.memset(fill0[:, :, :], 0))
            link(v.memset(fill0[:, :, FE + 1:FE + 2], -1))
            link(v.memset(fill1[:, :, :], 0))
            link(v.memset(fill1[:, :, 2:3], -1))
            v.memset(run[:, :, :], 0.0)
            v.memset(zeros[:, :], 0.0).then_inc(fill_ready, 1)
            v.memset(ones[:, :], 1.0)
            v.memset(ewsum[:, :], 0.0)
            v.memset(eps_ln[:, :], 1e-5)
            v.memset(rows[:, :, :, D:D + 1], 1.0)
            link(v.memset(hid[:, :, :, D:D + 1], 1.0))
            dve.wait_ge(pool_io, 1)
            v.tensor_copy(pidx[:, :], pidx_i[:, :])
            link(v.tensor_copy(iota[:, :], iota_i[:, :]))
            v.tensor_scalar(identb[:, :], iota[:, 0:P], pidx[:, 0:1], None, ALU.is_equal)
            v.tensor_scalar(ident[:, :], iota[:, 0:P], pidx[:, 0:1], None, ALU.is_equal)
            link(v.tensor_scalar(tri[:, :], iota[:, 0:P], pidx[:, 0:1], None, ALU.is_gt))
            dve.wait_ge(const_ld, const_total)

            def sort(r, ends):
                link(v.tensor_copy(slot_f[:, :], spare_i[:, :]))
                link(v.tensor_scalar(win_i[:, :], ends[:, :], 9, 2, ALU.logical_shift_right, ALU.logical_shift_left))
                link(v.tensor_scalar(low_i[:, :], ends[:, :], 3, None, ALU.bitwise_and))
                link(v.tensor_tensor(win_i[:, :], win_i[:, :], low_i[:, :], ALU.bitwise_or))
                link(v.tensor_copy(win_f[:, :], win_i[:, :]))
                link(v.tensor_scalar(low_i[:, :], ends[:, :], 2, P - 1, ALU.logical_shift_right, ALU.bitwise_and))
                if r == 0:
                    link(v.tensor_copy(field0[:, :, 0], dst_i[:, :]))
                    link(v.tensor_copy(field0[:, :, 1], low_i[:, :]))
                else:
                    link(v.memset(field1[:, :, :], 0))
                    link(v.tensor_scalar(win_i[:, :], src_i[:, :], 4, None, ALU.logical_shift_left))
                    link(v.tensor_tensor(field1[:, :, 0], win_i[:, :], ety_i[:, :], ALU.bitwise_or))
                    link(v.tensor_copy(field1[:, :, 1], src_i[:, :]))
                    link(v.tensor_copy(field1[:, :, 2], low_i[:, :]))
                n0 = chain.n
                with dve.Fori(0, NW) as w:
                    chain.n = n0 + w
                    link(v.tensor_scalar(scan_f[:, :], win_f[:, :], iota[:, bass.ds(w, 1)], 0.0, ALU.is_equal,
                                         ALU.add, accum_out=count[:, bass.ds(w, 1)]))
                chain.n = n0 + NW
                v.engine_nop().then_inc(counted, 1)
                dve.wait_ge(prefixed, r + 1)
                link(v.tensor_scalar(nblk_i[:, :], bank[7][:, 0:NW], float(G * P - 1), None, ALU.add))
                link(v.tensor_scalar(nblk_i[:, :], nblk_i[:, :], 8, None, ALU.logical_shift_right))
                link(v.tensor_scalar(nblk[:, :], nblk_i[:, :], 1.0, None, ALU.max))
                link(v.tensor_tensor_scan(bend[:, :], nblk[:, :], zeros[:, 0:NW], 0.0, ALU.add, ALU.add))
                link(v.tensor_tensor(bstart[:, :], bend[:, :], nblk[:, :], ALU.subtract))
                link(v.tensor_scalar(last_i[r][:, :], bend[:, :], -1.0, None, ALU.add))
                link(v.tensor_scalar(base[:, :], bstart[:, :], float(G * P), -1.0, ALU.mult, ALU.add))
                link(v.tensor_tensor(base[:, :], base[:, :], bank[6][:, 0:NW], ALU.add))
                link(v.memset(wofb[r][:, :], -1.0))
                link(v.memset(keep[r][:, :], 0.0))
                n0 = chain.n
                with dve.Fori(0, NW) as w:
                    chain.n = n0 + w * 4
                    link(v.scalar_tensor_tensor(wofb[r][:, :], iota[:, :], bstart[:, bass.ds(w, 1)], wofb[r][:, :],
                                                ALU.is_ge, ALU.add))
                    link(v.tensor_scalar(mask_i[:, :], win_f[:, :], iota[:, bass.ds(w, 1)], None, ALU.is_equal))
                    link(v.tensor_tensor_scan(scan_f[:, :], mask_i[:, :], zeros[:, 0:EC], base[:, bass.ds(w, 1)],
                                              ALU.add, ALU.add))
                    settle(dve)
                    link(v.copy_predicated(slot_f[:, :], mask_i[:, :], scan_f[:, :]))
                chain.n = n0 + 4 * NW
                link(v.tensor_tensor(keep[r][:, 1:NB], wofb[r][:, 1:NB], wofb[r][:, 0:NB - 1], ALU.is_equal))
                link(v.tensor_copy(win_i[:, :], slot_f[:, :]))
                link(v.tensor_scalar(low_i[:, :], win_i[:, :], P - 1, None, ALU.bitwise_and))
                link(v.tensor_scalar(win_i[:, :], win_i[:, :], 7, None, ALU.logical_shift_right))
                v.scalar_tensor_tensor(addr[r][:, :], low_i[:, :], float(PITCH), win_i[:, :], ALU.mult, ALU.add
                                       ).then_inc(sorted_, 1)

            sort(0, src_i)

            def layer_stats(c, src):
                for t in range(4):
                    ins = v.bn_stats(stat[:, t, :], src[:, t, :])
                c.link(dve, ins)
                settle(dve)
                for t in range(4):
                    ins = v.bn_aggr(mv[:, t, :], stat[:, t, :])
                return ins

            def layer_scale(c, done):
                c.link(dve, v.reciprocal(rstd[:, :], sd[:, :]))
                v.scalar_tensor_tensor(nmr[:, :], mv[:, :, 0], -1.0, rstd[:, :], ALU.mult, ALU.mult).then_inc(done, 1)

            c = ch["A0"]
            with dve.Fori(0, NQ) as q:
                c.begin(q)
                dve.wait_ge(ld["A0"], q * 16 + 16)
                layer_stats(c, xq).then_inc(A0d.sem, 1)
                dve.wait_ge(A0a.sem, A0a.after(q, "sd"))
                layer_scale(c, A0d.sem)
                dve.wait_ge(A0p.sem, A0p.after(q, "y"))
                v.tensor_tensor(yq[:, :, :], b4(1), row4(b1a_r), ALU.add).then_inc(A0d.sem, 1)
                c.end()

            sort(1, dst_i)
            dve.wait_ge(sorted_, 2)
            link(v.tensor_scalar(kpen[:, :], keep[1][:, :], -1.0, BIG, ALU.add, ALU.mult))
            link(v.tensor_scalar(woh[:, :], wofb[1][0:NW, :], pidx[0:NW, 0:1], None, ALU.is_equal))
            link(v.tensor_reduce(code[:, :], ident[0:3 * H, 0:3 * H].rearrange("p (s h) -> p h s", s=3),
                                 AX.X, ALU.add))
            link(v.tensor_copy(sel[:, :, :], code[:, :].unsqueeze(2).to_broadcast([3 * H, H, P])))
            link(v.tensor_scalar(pidx5[:, :], pidx_i[:, :], 5, None, ALU.logical_shift_right))
            link(v.tensor_copy(rn[:, :], pidx5[:, :]))
            link(v.tensor_scalar(hmask[:, :], iota[:, 0:H], rn[:, 0:1], None, ALU.is_equal))
            link(v.memset(gsel[:, 0, :], 0.0))
            link(v.memset(gsel[:, 1, :], 1.0))
            link(v.memset(gsel[:, 0, 0:1], 1.0))
            link(v.memset(gsel[:, 1, 0:1], 0.0))
            v.tensor_reduce(ewsum[0:125, :], ew[0:125, :], AX.X, ALU.add).then_inc(tw_sum, 1)
            dve.wait_ge(tw_tot, 1)
            link(v.tensor_scalar(gbias_c[:, :], bank[7][:, 0:1], 1.0 / E, None, ALU.mult))
            link(v.scalar_tensor_tensor(gbias_c[:, :], gbias_c[:, :], wg_last[:, 0:1], bgate_c[:, :],
                                        ALU.mult, ALU.add))
            link(v.tensor_scalar(ope[:, :], ope[:, :], 1.0, None, ALU.add))
            link(v.reciprocal(rn[:, :], lam[:, :]))
            link(v.tensor_scalar(rn[:, :], rn[:, :], 2.0, None, ALU.mult))
            for k in range(LAYERS):
                m = 1.0 if k == 0 else 2.0
                link(v.tensor_scalar(coef[:, 0, k:k + 1], rn[:, :], -m, None, ALU.mult))
                link(v.tensor_scalar(coef[:, 1, k:k + 1], rn[:, :], -1.0, m, ALU.add, ALU.mult))
                link(v.memset(coef[:, 2, k:k + 1], 0.0 if k == 0 else -1.0))

            dve.sem_inc(run_rdy, BODY)
            dve.sem_inc(E1d.sem, 2)
            dve.sem_inc(e0dve.sem, 1)
            dve.sem_inc(EBd.sem, 2)
            dve.sem_inc(T1td.sem, 2)

            def carry(r, i, j, which, psum, width):
                dve.wait_ge(hist_st[j], r * (16 * ITERS) + 16 + i * 16)
                dve.wait_ge(run_rdy, (r * NB + BODY) + i * BODY + j)
                v.scalar_tensor_tensor(run[:, j, 0:width], run[:, (j - 1) % BODY, 0:width],
                                       keep[which][:, bass.ds(i * BODY + j, 1)], psum, ALU.mult, ALU.add
                                       ).then_inc(run_rdy, 1)

            def one_hots(ring, g, col, r, i, pens=False):
                dve.wait_ge(rec_ld[g], r * (16 * (ITERS + 1)) + 16 + i * 16)
                for t in range(TG):
                    ins = v.tensor_scalar(onehot[:, g, t, :], iota[:, 0:P], ring[:, g, t, col:col + 1],
                                          None, ALU.is_equal)
                ins.then_inc(oh_rdy, 1)
                if pens:
                    for t in range(TG):
                        ins = v.tensor_scalar(pen[:, g, t, :], iota[:, 0:P], ring[:, g, t, col:col + 1],
                                              -BIG, ALU.not_equal, ALU.mult)
                    ins.then_inc(pen_rdy, 1)

            def groups(ring, col, r, use, pens=False):
                one_hots(ring, 0, col, r, 0, pens)
                with dve.Fori(0, ITERS) as i:
                    for g in range(GROUPS):
                        one_hots(ring, (g + 1) % GROUPS, col, r, i + (g + 1) // GROUPS, pens)
                        use(i, g, i * GROUPS + g)

            def two_ahead(ring, col, r, values, width, which):
                one_hots(ring, 0, col, r, 0)
                one_hots(ring, 1, col, r, 0)
                values(0, 0)

                def round_of(i, last):
                    for g in range(GROUPS):
                        if not (last and g == GROUPS - 1):
                            one_hots(ring, (g + 2) % GROUPS, col, r, i + (g + 2) // GROUPS)
                            values(i + (g + 1) // GROUPS, (g + 1) % GROUPS)
                        for b in range(2):
                            dve.wait_ge(summed, (r * NB + 1) + i * BODY + 2 * g + b)
                            carry(r, i, 2 * g + b, which, bank[2 + b][:, 0:width], width)

                with dve.Fori(0, ITERS - 1) as i:
                    round_of(i, False)
                round_of(ITERS - 1, True)

            def e0_values(i, g):
                k = i * GROUPS + g
                dve.wait_ge(gata[g], i * 64 + 64)
                dve.wait_ge(e0pe.sem, e0pe.after(k, "projected"))
                v.tensor_tensor(hpre[:, g % VALS, :, :], b4(1), rows[:, g, :, 0:D], ALU.add).then_inc(e0dve.sem, 1)

            two_ahead(rec0, FE + 1, 0, e0_values, D + 1, 0)

            c = ch["F0"]
            with dve.Fori(0, NQ) as q:
                c.begin(q)
                dve.wait_ge(ld["F0"], q * 96 + 96)
                v.tensor_scalar(ind[:, :], win_sum[:, :, D], 1.0, None, ALU.min)
                c.link(dve, v.tensor_scalar(cn[:, :], win_sum[:, :, D], 1.0, None, ALU.max))
                c.link(dve, v.reciprocal(rc[:, :], cn[:, :]))
                v.tensor_tensor(aq[:, :, :], win_sum[:, :, 0:D], over(rc[:, :]), ALU.mult).then_inc(F0d.sem, 1)
                dve.wait_ge(F0p.sem, F0p.after(q, "agg"))
                for t in range(4):
                    ins = v.scalar_tensor_tensor(yq[:, t, :], b1b_r[:, :], ind[:, t:t + 1], b4(2)[:, t, :],
                                                 ALU.mult, ALU.add)
                ins.then_inc(F0d.sem, 1)
                dve.wait_ge(F0p.sem, F0p.after(q, "o"))
                c.link(dve, v.tensor_tensor(xo[:, :, :], b4(2), xq[:, :, :], ALU.add))
                c.link(dve, v.tensor_tensor(xo[:, :, :], xo[:, :, :], row4(b2b_r), ALU.add))
                layer_stats(c, xo).then_inc(F0d.sem, 1)
                dve.wait_ge(F0a.sem, F0a.after(q, "sd"))
                layer_scale(c, F0d.sem)
                c.end()

            with dve.Fori(0, LAYERS) as l:
                dve.wait_ge(layer_ld, l * 128 + 128)
                v.tensor_scalar(amat[:, 0:H], hmask[:, :], acol[:, 0:1], None, ALU.mult)
                v.tensor_scalar(amat[:, H:2 * H], hmask[:, :], acol[:, 1:2], None, ALU.mult)
                dve.wait_ge(wT_ready, l * 2 + 1)
                v.tensor_copy(wgatT[:, :], bank[0][:, 0:P]).then_inc(attw_ready, 1)
                dve.wait_ge(wT_ready, l * 2 + 2)
                v.tensor_copy(wgat[:, D:D + 2 * H], bank[1][:, 0:2 * H]).then_inc(attw_ready, 1)

                c = ch["T1"]
                with dve.Fori(0, NQ) as q:
                    rnd = l * NQ + q
                    c.begin(rnd)
                    dve.wait_ge(T1p.sem, T1p.after(rnd, "z"))
                    v.tensor_copy(zq[:, 0:2, :], bank[4][:, 0:2 * (FZ + H)].rearrange("p (t f) -> p t f", t=2))
                    c.link(dve, v.tensor_copy(zq[:, 2:4, :],
                                              bank[5][:, 0:2 * (FZ + H)].rearrange("p (t f) -> p t f", t=2)))
                    c.link(dve, v.tensor_copy(el3[:, :, 0:H], zq[:, :, D:D + H]))
                    c.link(dve, v.tensor_tensor(elr[:, :, :], zq[:, :, D:D + H], el3[:, :, 0:H], ALU.subtract))
                    c.link(dve, v.tensor_copy(el3[:, :, H:2 * H], elr[:, :, :]))
                    c.link(dve, v.tensor_tensor(elr[:, :, :], elr[:, :, :], el3[:, :, H:2 * H], ALU.subtract))
                    then(T1d, v.tensor_copy(el3[:, :, 2 * H:3 * H], elr[:, :, :]), rnd, "z")
                    c.end()
                    for t in range(4):
                        s = t % 2
                        dve.wait_ge(st_tab[s], (rnd * 2 + t // 2) * 16 + 16)
                        v.tensor_copy(tabq[s][:, :, D:KT].bitcast(BF16),
                                      el3[:, t, :].unsqueeze(1).to_broadcast([P, R, 3 * H]))
                        for j in (2, 3):
                            dve.wait_ge(T1tp.sem, (rnd * 4 + t) * 4 + j + 1)
                            v.tensor_copy(tabq[s][:, 4 * j:4 * j + 4, 0:D], b4(j)).then_inc(T1td.sem, 1)

                def use_e1a(i, g, k):
                    for b in range(2):
                        n = l * NGR + k
                        dve.wait_ge(E1p.sem, E1p.after(n, f"max{b}"))
                        v.tensor_reduce(bmax[:, bass.ds(i * BODY + 2 * g + b, 1), :].rearrange("p b h -> p (b h)"),
                                        psum[:, 4 + 2 * b:6 + 2 * b, :].rearrange("p b (h e) -> p h b e", h=H),
                                        AX.XY, ALU.max).then_inc(E1d.sem, 1)
                        dve.wait_ge(summed, (l * 2 + 1) * NB + k * 2 + b + 1)
                        carry(l * 2 + 1, i, 2 * g + b, 1, bank[2 + b][:, 0:D], D)

                groups(rec1, 2, l * 2 + 1, use_e1a, pens=True)

                c = ch["M"]
                c.begin(l)
                dve.wait_ge(E1d.sem, (l + 1) * (2 * NGR) + 2)
                settle(dve)
                for h in range(H):
                    c.link(dve, v.tensor_tensor_scan(wmax[:, :, h], kpen[:, :], bmax[:, :, h], -BIG, ALU.add, ALU.max))
                c.link(dve, v.tensor_copy(bmax[:, NB - 1, :], wmax[:, NB - 1, :]))
                for h in range(H):
                    c.link(dve, v.tensor_tensor_scan(bmax[:, NB - 2::-1, h], kpen[:, NB - 1:0:-1],
                                                     wmax[:, NB - 2::-1, h], wmax[:, NB - 1, h:h + 1],
                                                     ALU.add, ALU.max))
                dve.wait_ge(Mp.sem, Mp.after(l, "er"))
                c.link(dve, v.tensor_copy(erm[:, :, 0:H].rearrange("p b h -> p h b"), psum[:, 0:H, 0:NB]))
                c.link(dve, v.tensor_tensor(erm[:, :, H:2 * H], bmax[:, :, :], erm[:, :, 0:H], ALU.add))
                c.link(dve, v.scalar_tensor_tensor(erm[:, :, H:2 * H], erm[:, :, H:2 * H], 0.2, erm[:, :, H:2 * H],
                                                   ALU.mult, ALU.max))
                c.link(dve, v.tensor_copy(erm3[:, :, 0:8], erm[:, :, :]))
                c.link(dve, v.tensor_tensor(rest[:, :, :], erm[:, :, :], erm3[:, :, 0:8], ALU.subtract))
                c.link(dve, v.tensor_copy(erm3[:, :, 8:16], rest[:, :, :]))
                c.link(dve, v.tensor_tensor(rest[:, :, :], rest[:, :, :], erm3[:, :, 8:16], ALU.subtract))
                v.tensor_copy(erm3[:, :, 16:24], rest[:, :, :]).then_inc(Md.sem, 1)
                c.end()

                def e1b_values(i, g):
                    n = i * GROUPS + g + l * NGR
                    c = ch["E1b"]
                    c.begin(n)
                    dve.wait_ge(EBp.sem, EBp.after(n, "erm"))
                    c.link(dve, v.tensor_reduce(erme[:, :, :],
                                                bank[1][:, 0:TG * 24].rearrange("p (t s c) -> p t c s", t=TG, s=3),
                                                AX.X, ALU.add))
                    dve.wait_ge(gatz[g], l * (64 * ITERS) + 64 + i * 64)
                    c.link(dve, v.tensor_tensor(att[:, :, :], zrow[:, g, :, D:FZ], erme[:, :, 0:H], ALU.add))
                    c.link(dve, v.scalar_tensor_tensor(att[:, :, :], att[:, :, :], 0.2, att[:, :, :],
                                                       ALU.mult, ALU.max))
                    c.link(dve, v.tensor_tensor(att[:, :, :], att[:, :, :], erme[:, :, H:2 * H], ALU.subtract))
                    c.end()
                    v.tensor_scalar(att[:, :, :], att[:, :, :], 0.0, None, ALU.min).then_inc(EBd.sem, 1)
                    dve.wait_ge(EBa.sem, EBa.after(n, "exp"))
                    v.tensor_tensor(zex[:, g % VALS, :, 0:D].rearrange("p t (h d) -> p t h d", h=H),
                                    zrow[:, g, :, 0:D].rearrange("p t (h d) -> p t h d", h=H),
                                    zex[:, g % VALS, :, D:FZ].unsqueeze(3).to_broadcast([P, TG, H, DH]),
                                    ALU.mult).then_inc(EBd.sem, 1)

                two_ahead(rec1, 2, l * 2 + 2, e1b_values, FZ, 1)

                c = ch["F1"]
                with dve.Fori(0, NQ) as q:
                    rnd = l * NQ + q
                    c.begin(rnd)
                    dve.wait_ge(ld["F1"], rnd * 144 + 144)
                    c.link(dve, v.tensor_scalar(den[:, :, :], win_sum[:, :, D:FZ], 1e-30, None, ALU.max))
                    c.link(dve, v.reciprocal(den[:, :, :], den[:, :, :]))
                    v.tensor_tensor(yq[:, :, :].rearrange("p t (h d) -> p t h d", h=H),
                                    win_sum[:, :, 0:D].rearrange("p t (h d) -> p t h d", h=H),
                                    den[:, :, :].unsqueeze(3).to_broadcast([P, 4, H, DH]), ALU.mult
                                    ).then_inc(F1d.sem, 1)
                    dve.wait_ge(F1a.sem, F1a.after(rnd, "gate"))
                    c.link(dve, v.tensor_scalar(tE[:, :, :], tE[:, :, :], gsel[:, 0, bass.ds(l, 1)],
                                                gsel[:, 1, bass.ds(l, 1)], ALU.mult, ALU.add))
                    c.link(dve, v.tensor_tensor(tE[:, :, :], tE[:, :, :], tD[:, :, :], ALU.mult))
                    v.tensor_scalar(xo[:, :, :], tE[:, :, :], 0.0, None, ALU.max).then_inc(F1d.sem, 1)
                    c.end()

            c = ch["A2"]
            with dve.Fori(0, NQ) as q:
                c.begin(q)
                dve.wait_ge(ld["A2"], q * 32 + 32)
                dve.wait_ge(A2p.sem, A2p.after(q, "T"))
                c.link(dve, v.tensor_tensor(xo[:, :, :], b4(0), xq[:, :, :], ALU.add))
                layer_stats(c, xo).then_inc(A2d.sem, 1)
                dve.wait_ge(A2a.sem, A2a.after(q, "sd"))
                layer_scale(c, A2d.sem)
                c.end()

            def use_gather(r, k0):
                def use(i, g, k):
                    for b in range(2):
                        dve.wait_ge(summed, r * NB + k * 2 + b + 1)
                        carry(r, i, 2 * g + b, 1, bank[2 + b][:, 0:D + 1], D + 1)
                return use

            groups(rec1, 2, 7, use_gather(7, 0))
            dve.wait_ge(wT_ready, 7)
            v.tensor_copy(w1T[:, :], bank[0][:, 0:P])
            v.tensor_copy(w2T[:, :], bank[0][:, P:2 * P]).then_inc(attw_ready, 1)
            with dve.Fori(0, NQ) as q:
                dve.wait_ge(ld["F2"], q * 80 + 80)
                v.tensor_scalar(cn[:, :], win_sum[:, :, D], 1.0, None, ALU.max).then_inc(F2d.sem, 1)
                v.scalar_tensor_tensor(yq[:, :, :], hq[:, :, :], ope[:, 0:1], win_sum[:, :, 0:D], ALU.mult, ALU.add
                                       ).then_inc(F2d.sem, 1)
                dve.wait_ge(F2a.sem, F2a.after(q, "sd"))
                v.reciprocal(dinv[:, bass.ds(q * 4, 4)], sd[:, :])
            dve.wait_ge(F2a.sem, NQ * 3)
            with dve.Fori(0, N // 512) as q:
                v.bn_stats(bnst[:, bass.ds(q, 1), :].rearrange("p a b -> p (a b)"), uT[:, bass.ds(q * 512, 512)])
            lastq = uT[:, (NQ - 1) * 512:NQ * 512].rearrange("p (t n) -> p t n", t=4)
            left = N - (NQ - 1) * 512
            full, more = divmod(left, 4)
            v.bn_stats(bnst[:, NQ - 1, :], lastq[:, 0:more, 0:full + 1])
            link(v.bn_stats(bnst[:, NQ, :], lastq[:, more:4, 0:full]))
            v.bn_aggr(bnmv[:, :], bnst[:, :, :]).then_inc(bnorm, 1)
            dve.wait_ge(bnorm, 2)
            link(v.reciprocal(bnr[:, :], bnsd[:, :]))
            link(v.tensor_tensor(bnscale[:, :], bnr[:, :], gamma_c[:, :], ALU.mult))
            link(v.tensor_tensor(bnshift[:, :], bnmv[:, 0:1], bnscale[:, :], ALU.mult))
            v.tensor_tensor(bnshift[:, :], beta_c[:, :], bnshift[:, :], ALU.subtract).then_inc(bnorm, 1)
            c = ch["B2"]
            with dve.Fori(0, NQ) as q:
                c.begin(q)
                dve.wait_ge(ld["B2"], q * 32 + 32)
                dve.wait_ge(B2p.sem, B2p.after(q, "y"))
                c.link(dve, v.tensor_tensor(yq[:, :, :], b4(0), row4(b2_r), ALU.add))
                c.link(dve, v.scalar_tensor_tensor(yq[:, :, :], yq[:, :, :], 0.0, hq[:, :, :], ALU.max, ALU.add))
                c.link(dve, v.tensor_tensor(xo[:, :, :], yq[:, :, :], xq[:, :, :], ALU.add))
                layer_stats(c, xo).then_inc(B2d.sem, 1)
                dve.wait_ge(B2a.sem, B2a.after(q, "sd"))
                layer_scale(c, B2d.sem)
                dve.wait_ge(B2a.sem, B2a.after(q, "h"))
                v.tensor_tensor(yq[:, :, :], ho[:, :, :], over(dinv[:, bass.ds(q * 4, 4)]), ALU.mult
                                ).then_inc(B2d.sem, 1)
                dve.wait_ge(B2p.sem, B2p.after(q, "acc"))
                v.tensor_copy(aq[:, :, :], b4(2)).then_inc(B2d.sem, 1)
                c.end()
            with dve.Fori(0, LAYERS) as k:
                groups(rec1, 2, k + 8, use_gather(k + 8, 0))
                c = ch["F3"]
                with dve.Fori(0, NQ) as q:
                    rnd = k * NQ + q
                    c.begin(rnd)
                    dve.wait_ge(ld["F3"], rnd * 112 + 112)
                    c.link(dve, v.tensor_tensor(tD[:, :, :], win_sum[:, :, 0:D], over(dinv[:, bass.ds(q * 4, 4)]),
                                                ALU.mult))
                    c.link(dve, v.tensor_scalar(tE[:, :, :], tD[:, :, :], coef[:, 0, bass.ds(k, 1)], None, ALU.mult))
                    c.link(dve, v.scalar_tensor_tensor(tE[:, :, :], hq[:, :, :], coef[:, 1, bass.ds(k, 1)],
                                                       tE[:, :, :], ALU.mult, ALU.add))
                    c.end()
                    then(F3d, v.scalar_tensor_tensor(xo[:, :, :], xq[:, :, :], coef[:, 2, bass.ds(k, 1)],
                                                     tE[:, :, :], ALU.mult, ALU.add), rnd, "x")
                    v.tensor_tensor(yq[:, :, :], xo[:, :, :], over(dinv[:, bass.ds(q * 4, 4)]), ALU.mult
                                    ).then_inc(F3d.sem, 1)
                    dve.wait_ge(F3p.sem, F3p.after(rnd, "acc"))
                    v.tensor_tensor(ho[:, :, :], b4(1), aq[:, :, :], ALU.add).then_inc(F3d.sem, 1)
            with dve.Fori(0, NQ) as q:
                dve.wait_ge(ld["O"], q * 32 + 32)
                v.tensor_tensor(hq[:, :, :], aq[:, :, :], row4(b3_r), ALU.add).then_inc(ch["O"].sem, 1)
                dve.wait_ge(ch["O"].sem, q * 2 + 1)
                v.scalar_tensor_tensor(xo[:, :, :], hq[:, :, :], 0.0, xq[:, :, :], ALU.max, ALU.add
                                       ).then_inc(ch["O"].sem, 1)

        @block.scalar
        def _(act):
            s = nc.scalar

            def sqrt4(src, done):
                s.activation(sd[:, :], src, ACT.Sqrt, bias=eps_ln[:, 0:1]).then_inc(done, 1)

            def normalise(src, dst):
                for t in range(4):
                    ins = s.activation(dst[:, t, :], src[:, t, :], ACT.Relu, bias=nmr[:, t:t + 1], scale=rstd[:, t:t + 1])
                return ins

            with act.Fori(0, NQ) as q:
                act.wait_ge(A0d.sem, A0d.after(q, "stats"))
                sqrt4(mv[:, :, 1], A0a.sem)
                act.wait_ge(A0d.sem, A0d.after(q, "ln"))
                normalise(xq, ho).then_inc(A0a.sem, 1)
                act.wait_ge(A0p.sem, A0p.after(q, "hT"))
                s.copy(tA[:, :, :], b4(0)).then_inc(A0a.sem, 1)

            def pay(r, field, dst):
                act.wait_ge(sorted_, r + 1)
                with act.Fori(0, EC // (2 * CH)) as k:
                    for h in range(2):
                        act.wait_ge(scat[h], r * (128 * (EC // (2 * CH))) + 16 + k * 128)
                        if r == 0:
                            act.wait_ge(pay_ld[h], k * 48 + 48)
                        c = (2 * k + h) * CH
                        s.copy(dst[:, h, :, :], field[:, bass.ds(c, CH), :])
                        s.copy(payaddr[:, h, :], addr[r][:, bass.ds(c, CH)]).then_inc(pay_rdy, 1)

            pay(0, field0, pay0[:, :, :, FE:FE + 2])
            pay(1, field1, pay1)

            with act.Fori(0, ITERS) as i:
                for g in range(GROUPS):
                    k = i * GROUPS + g
                    act.wait_ge(e0pe.sem, e0pe.after(k, "turned"))
                    s.copy(eaT[:, :, :], bank[0][0:FE, :].rearrange("p (t e) -> p t e", t=TG)).then_inc(e0act.sem, 1)
                    act.wait_ge(e0dve.sem, e0dve.after(k + 1, "added"))
                    s.activation(hid[:, g % VALS, :, 0:D], hpre[:, g % VALS, :, :], ACT.Relu).then_inc(e0act.sem, 1)

            with act.Fori(0, NQ) as q:
                act.wait_ge(F0p.sem, F0p.after(q, "T"))
                s.copy(tA[:, :, :], b4(0))
                s.copy(tB[:, :, :], b4(1)).then_inc(F0a.sem, 1)
                act.wait_ge(F0p.sem, F0p.after(q, "agT"))
                s.copy(tA[:, :, :], b4(0)).then_inc(F0a.sem, 1)
                act.wait_ge(F0p.sem, F0p.after(q, "u"))
                s.activation(tC[:, :, :], b4(3), ACT.Relu, bias=b2a_c[:, 0:1]).then_inc(F0a.sem, 1)
                act.wait_ge(F0d.sem, F0d.after(q, "stats"))
                sqrt4(mv[:, :, 1], F0a.sem)
                act.wait_ge(F0d.sem, F0d.after(q, "ln"))
                normalise(xo, ho).then_inc(F0a.sem, 1)
                act.wait_ge(F0p.sem, F0p.after(q, "h1T"))
                s.copy(tC[:, :, :], b4(0)).then_inc(F0a.sem, 1)

            act.sem_inc(T1ta.sem, 2)
            with act.Fori(0, LAYERS) as l:
                with act.Fori(0, NQ) as q:
                    rnd = l * NQ + q
                    for t in range(4):
                        act.wait_ge(st_tab[t % 2], (rnd * 2 + t // 2) * 16 + 16)
                        for j in (0, 1):
                            act.wait_ge(T1tp.sem, (rnd * 4 + t) * 4 + j + 1)
                            s.copy(tabq[t % 2][:, 4 * j:4 * j + 4, 0:D], b4(j)).then_inc(T1ta.sem, 1)
                with act.Fori(0, NGR) as k:
                    n = l * NGR + k
                    act.wait_ge(E1p.sem, E1p.after(n, "elT"))
                    s.copy(elT[:, :, :], bank[1].bitcast(BF16)[0:3 * H, 0:TG * P].rearrange("p (t e) -> p t e", t=TG)
                           ).then_inc(E1a.sem, 1)
                with act.Fori(0, ITERS) as i:
                    for g in range(GROUPS):
                        n = i * GROUPS + g + l * NGR
                        act.wait_ge(EBp.sem, EBp.after(n, "ohT"))
                        s.copy(ohT[:, :, :], b4(0)).then_inc(EBa.sem, 1)
                        act.wait_ge(EBd.sem, EBd.after(n + 1, "logits"))
                        s.activation(zex[:, g % VALS, :, D:FZ], att[:, :, :], ACT.Exp).then_inc(EBa.sem, 1)
                with act.Fori(0, NQ) as q:
                    rnd = l * NQ + q
                    act.wait_ge(F1p.sem, F1p.after(rnd, "T"))
                    s.activation(tB[:, :, :], b4(0), ACT.Identity, bias=brel_c[:, 0:1]).then_inc(F1a.sem, 1)
                    s.activation(tC[:, :, :], b4(1), ACT.Identity, bias=bgat_c[:, 0:1]).then_inc(F1a.sem, 1)
                    act.wait_ge(F1p.sem, F1p.after(rnd, "hc"))
                    s.activation(tD[:, :, :], b4(2), ACT.Identity, bias=bfuse_c[:, 0:1]).then_inc(F1a.sem, 1)
                    act.wait_ge(F1p.sem, F1p.after(rnd, "gate"))
                    s.activation(tE[:, :, :], b4(3), ACT.Sigmoid, bias=gbias_c[:, 0:1]).then_inc(F1a.sem, 1)
            with act.Fori(0, NQ) as q:
                act.wait_ge(A2d.sem, A2d.after(q, "stats"))
                sqrt4(mv[:, :, 1], A2a.sem)
                act.wait_ge(A2d.sem, A2d.after(q, "ln"))
                normalise(xo, ho).then_inc(A2a.sem, 1)
            with act.Fori(0, NQ) as q:
                act.wait_ge(F2d.sem, F2d.after(q, "cn"))
                s.activation(sd[:, :], cn[:, :], ACT.Sqrt).then_inc(F2a.sem, 1)
                act.wait_ge(F2p.sem, F2p.after(q, "T"))
                s.copy(tA[:, :, :], b4(1)).then_inc(F2a.sem, 1)
                act.wait_ge(F2p.sem, F2p.after(q, "u"))
                s.activation(uT[:, bass.ds(q * 512, 512)], bank[2], ACT.Identity, bias=b1_c[:, 0:1]
                             ).then_inc(F2a.sem, 1)
            act.wait_ge(bnorm, 1)
            s.activation(bnsd[:, :], bnmv[:, 1:2], ACT.Sqrt, bias=eps_ln[:, 0:1]).then_inc(bnorm, 1)
            act.wait_ge(bnorm, 3)
            with act.Fori(0, NQ) as q:
                s.activation(tA[:, :, :].rearrange("p t f -> p (t f)"), uT[:, bass.ds(q * 512, 512)], ACT.Relu,
                             bias=bnshift[:, 0:1], scale=bnscale[:, 0:1]).then_inc(B2a.sem, 1)
                act.wait_ge(B2d.sem, B2d.after(q, "stats"))
                sqrt4(mv[:, :, 1], B2a.sem)
                act.wait_ge(B2d.sem, B2d.after(q, "ln"))
                normalise(xo, ho).then_inc(B2a.sem, 1)
                act.wait_ge(B2p.sem, B2p.after(q, "T"))
                s.copy(tB[:, :, :], b4(1)).then_inc(B2a.sem, 1)
            with act.Fori(0, LAYERS * NQ) as rnd:
                act.wait_ge(F3p.sem, F3p.after(rnd, "T"))
                s.copy(tA[:, :, :], b4(0)).then_inc(F3a.sem, 1)

        @block.tensor
        def _(pe):
            mm = nc.tensor.matmul

            def flat(t):
                return t[:, :, :].rearrange("p t f -> p (t f)")

            def turn(dst, src):
                for t in range(4):
                    ins = nc.tensor.transpose(dst[:, t, :], src[:, t, :], ident[:, :])
                return ins

            def rows_times(j, lhs, rhs):
                for t in range(4):
                    ins = mm(b4(j)[:, t, :], lhs[:, t, :], rhs, start=True, stop=True)
                return ins

            def prefix(r):
                pe.wait_ge(counted, r + 1)
                mm(bank[6][:, 0:NW], tri[:, :], count[:, :], start=True, stop=True)
                mm(bank[7][:, 0:NW], ones[:, :], count[:, :], start=True, stop=True).then_inc(prefixed, 1)

            prefix(0)
            with pe.Fori(0, NQ) as q:
                pe.wait_ge(A0a.sem, A0a.after(q, "h"))
                turn(b4(0), ho).then_inc(A0p.sem, 1)
                pe.wait_ge(A0a.sem, A0a.after(q, "hT"))
                rows_times(1, tA, w1a_x[:, :]).then_inc(A0p.sem, 1)
            prefix(1)
            pe.wait_ge(tw_sum, 1)
            mm(bank[7][:, 0:1], ones[:, :], ewsum[:, :], start=True, stop=True).then_inc(tw_tot, 1)

            def block_sums(r, k, g, b, src, width):
                pe.wait_ge(run_rdy, r * NB + (BODY - 1) + k * 2 + b)
                for t in range(G):
                    ins = mm(bank[2 + b][:, 0:width], onehot[:, g, 2 * b + t, :], src[:, 2 * b + t, 0:width],
                             start=(t == 0), stop=(t == G - 1))
                ins.then_inc(summed, 1)

            def one_hots_ready(r, k):
                pe.wait_ge(oh_rdy, r * (NGR + 1) + 1 + k)

            def one_ahead(r, prepare, values_ready, src, width):
                prepare(0, 0)

                def round_of(i, last):
                    for g in range(GROUPS):
                        if not (last and g == GROUPS - 1):
                            prepare(i + (g + 1) // GROUPS, (g + 1) % GROUPS)
                        k = i * GROUPS + g
                        one_hots_ready(r, k)
                        values_ready(k)
                        for b in range(2):
                            block_sums(r, k, g, b, src[:, g % VALS], width)

                with pe.Fori(0, ITERS - 1) as i:
                    round_of(i, False)
                round_of(ITERS - 1, True)

            def e0_prepare(i, g):
                k = i * GROUPS + g
                pe.wait_ge(rec_ld[g], 16 + i * 16)
                settle(pe)
                for t in range(TG):
                    ins = nc.tensor.transpose(bank[0][0:FE, t * P:(t + 1) * P],
                                              rec0[:, g, t, 0:FE].bitcast(F32), ident[:, :])
                ins.then_inc(e0pe.sem, 1)
                pe.wait_ge(e0act.sem, e0act.after(k, "turned"))
                pe.wait_ge(e0dve.sem, k + 1)
                rows_times(1, eaT, w1a_e[:, :]).then_inc(e0pe.sem, 1)

            def e0_relu(k):
                pe.wait_ge(e0act.sem, e0act.after(k, "relu"))

            one_ahead(0, e0_prepare, e0_relu, hid, D + 1)

            with pe.Fori(0, NQ) as q:
                pe.wait_ge(ld["F0"], q * 96 + 96)
                pe.wait_ge(F0d.sem, F0d.after(q, "sm"))
                turn(b4(0), aq)
                turn(b4(1), hq).then_inc(F0p.sem, 1)
                pe.wait_ge(F0a.sem, F0a.after(q, "T"))
                rows_times(2, tA, w1b[:, :]).then_inc(F0p.sem, 1)
                pe.wait_ge(F0d.sem, F0d.after(q, "agg"))
                turn(b4(0), yq).then_inc(F0p.sem, 1)
                pe.wait_ge(F0a.sem, F0a.after(q, "agT"))
                mm(bank[3], w2a[:, 0, :], flat(tB), start=True, stop=False)
                mm(bank[3], w2a[:, 1, :], flat(tA), start=False, stop=True).then_inc(F0p.sem, 1)
                pe.wait_ge(F0a.sem, F0a.after(q, "u"))
                rows_times(2, tC, w2b[:, :]).then_inc(F0p.sem, 1)
                pe.wait_ge(F0a.sem, F0a.after(q, "h"))
                turn(b4(0), ho).then_inc(F0p.sem, 1)

            with pe.Fori(0, LAYERS) as l:
                pe.wait_ge(layer_ld, l * 128 + 128)
                nc.tensor.transpose(bank[0][:, 0:P], wgat[:, 0:D], ident[:, :]).then_inc(wT_ready, 1)
                pe.wait_ge(attw_ready, l * 2 + 1)
                mm(bank[1][:, 0:2 * H], wgatT[:, :], amat[:, :], start=True, stop=True).then_inc(wT_ready, 1)
                pe.wait_ge(attw_ready, l * 2 + 2)
                settle(pe)
                with pe.Fori(0, NQ) as q:
                    rnd = l * NQ + q
                    pe.wait_ge(ld["T1"], rnd * 16 + 16)
                    for t in range(4):
                        ins = mm(bank[4 + t // 2][:, (t % 2) * (FZ + H):(t % 2 + 1) * (FZ + H)], tA[:, t, :],
                                 wgat[:, :], start=True, stop=True)
                    ins.then_inc(T1p.sem, 1)
                    for t in range(4):
                        for j in range(4):
                            pe.wait_ge((T1ta, T1td)[j // 2].sem, (rnd * 4 + t) * 2 + j % 2 + 1)
                            mm(bank[j], tA[:, t, :], wrel[:, 4 * j:4 * j + 4, :].rearrange("p r f -> p (r f)"),
                               start=True, stop=True).then_inc(T1tp.sem, 1)
                with pe.Fori(0, ITERS) as i:
                    for g in range(GROUPS):
                        k = i * GROUPS + g
                        n = l * NGR + k
                        pe.wait_ge(gata[g], (l * ITERS + ITERS + 1) * 64 + i * 64)
                        for t in range(TG):
                            ins = nc.tensor.transpose(bank[1].bitcast(BF16)[0:3 * H, t * P:(t + 1) * P],
                                                      rows1[:, g, t, D:KT].bitcast(BF16), identb[:, :])
                        ins.then_inc(E1p.sem, 1)
                        one_hots_ready(l * 2 + 1, k)
                        pe.wait_ge(pen_rdy, l * (NGR + 1) + 1 + k)
                        for b in range(2):
                            block_sums(l * 2 + 1, k, g, b, rows1[:, g], D)
                            if b == 0:
                                pe.wait_ge(E1a.sem, E1a.after(n, "elT"))
                            pe.wait_ge(E1d.sem, E1d.after(n, f"max{b}"))
                            for t in range(2 * b, 2 * b + 2):
                                mm(bank[4 + t], pen[:, g, t, :], identb[:, :].unsqueeze(1).to_broadcast([P, H, P]),
                                   start=True, stop=False)
                                for h in range(H):
                                    ins = mm(bank[4 + t][:, h * P:(h + 1) * P], sel[:, h, :], elT[:, t, :],
                                             start=False, stop=(h == H - 1))
                            ins.then_inc(E1p.sem, 1)
                pe.wait_ge(ld["M"], l * 16 + 16)
                for h in range(H):
                    ins = mm(bank[h][:, 0:NB], erw[:, :, h], woh[:, :], start=True, stop=True)
                ins.then_inc(Mp.sem, 1)
                pe.wait_ge(Md.sem, Md.after(l, "erm3"))
                settle(pe)
                def e1b_prepare(i, g):
                    k = i * GROUPS + g
                    n = i * GROUPS + g + l * NGR
                    one_hots_ready(l * 2 + 2, k)
                    turn(b4(0), onehot[:, g]).then_inc(EBp.sem, 1)
                    pe.wait_ge(EBa.sem, EBa.after(n, "ohT"))
                    pe.wait_ge(EBd.sem, EBd.after(n, "logits"))
                    for t in range(TG):
                        ins = mm(bank[1][:, t * 24:(t + 1) * 24], ohT[:, t, :],
                                 erm3[:, bass.ds(i * BODY + (2 * g + t // 2), 1), :].rearrange("p b c -> p (b c)"),
                                 start=True, stop=True)
                    ins.then_inc(EBp.sem, 1)

                def e1b_weighted(k):
                    pe.wait_ge(EBd.sem, EBd.after(k + l * NGR + 1, "weighted"))

                one_ahead(l * 2 + 2, e1b_prepare, e1b_weighted, zex, FZ)
                with pe.Fori(0, NQ) as q:
                    rnd = l * NQ + q
                    pe.wait_ge(ld["F1"], rnd * 144 + 144)
                    mm(bank[0], wloop[:, :], flat(tA), start=True, stop=False)
                    for t in range(4):
                        mm(b4(0)[:, t, :], aq[:, t, :], ident[:, :], start=False, stop=(t == 3))
                    pe.wait_ge(F1d.sem, F1d.after(rnd, "mean"))
                    turn(b4(1), yq).then_inc(F1p.sem, 1)
                    pe.wait_ge(F1a.sem, F1a.after(rnd, "gat"))
                    mm(bank[2], wfuse[:, 0, :], flat(tB), start=True, stop=False)
                    mm(bank[2], wfuse[:, 1, :], flat(tC), start=False, stop=True).then_inc(F1p.sem, 1)
                    pe.wait_ge(F1a.sem, F1a.after(rnd, "hc"))
                    mm(bank[3], wgate[:, :], flat(tD), start=True, stop=True).then_inc(F1p.sem, 1)

            with pe.Fori(0, NQ) as q:
                pe.wait_ge(ld["A2"], q * 32 + 32)
                turn(b4(0), tA).then_inc(A2p.sem, 1)

            def gather_sums(r, base):
                with pe.Fori(0, ITERS) as i:
                    for g in range(GROUPS):
                        k = i * GROUPS + g
                        one_hots_ready(r, k)
                        pe.wait_ge(gatx[g], (base * ITERS + 1) * 64 + i * 64)
                        for b in range(2):
                            block_sums(r, k, g, b, rows[:, g], D + 1)

            gather_sums(7, 0)
            pe.wait_ge(run_rdy, 8 * NB + BODY)
            nc.tensor.transpose(bank[0][:, 0:P], w12[:, 0, :], ident[:, :])
            nc.tensor.transpose(bank[0][:, P:2 * P], w12[:, 1, :], ident[:, :]).then_inc(wT_ready, 1)
            pe.wait_ge(attw_ready, 7)
            with pe.Fori(0, NQ) as q:
                pe.wait_ge(F2d.sem, F2d.after(q, "pre"))
                turn(b4(1), yq).then_inc(F2p.sem, 1)
                pe.wait_ge(F2a.sem, F2a.after(q, "T"))
                mm(bank[2], w1T[:, :], flat(tA), start=True, stop=True).then_inc(F2p.sem, 1)
            with pe.Fori(0, NQ) as q:
                pe.wait_ge(B2a.sem, B2a.after(q, "v"))
                rows_times(0, tA, w2T[:, :]).then_inc(B2p.sem, 1)
                pe.wait_ge(B2a.sem, B2a.after(q, "h"))
                turn(b4(1), ho).then_inc(B2p.sem, 1)
                pe.wait_ge(B2a.sem, B2a.after(q, "T"))
                rows_times(2, tB, w3[:, 0, :]).then_inc(B2p.sem, 1)
            with pe.Fori(0, LAYERS) as k:
                gather_sums(k + 8, k + 1)
                with pe.Fori(0, NQ) as q:
                    rnd = k * NQ + q
                    pe.wait_ge(F3d.sem, F3d.after(rnd, "x"))
                    turn(b4(0), xo).then_inc(F3p.sem, 1)
                    pe.wait_ge(F3a.sem, F3a.after(rnd, "T"))
                    rows_times(1, tA, w3[:, bass.ds(k + 1, 1), :].rearrange("p a f -> p (a f)")).then_inc(F3p.sem, 1)


INS = ['x', 'src', 'dst', 'edge_attr_64', 'edge_type_16', 'edge_weight', 'L0_gnn_u', 'L0_gnn_W1a', 'L0_gnn_b1a',
       'L0_gnn_W1b', 'L0_gnn_b1b', 'L0_gnn_W2a', 'L0_gnn_b2a', 'L0_gnn_W2b', 'L0_gnn_b2b', 'L1_gnn_W_rel',
       'L1_gnn_b_rel', 'L1_gnn_W_loop', 'L1_gnn_W_gat', 'L1_gnn_attn_l', 'L1_gnn_attn_r', 'L1_gnn_b_gat',
       'L1_gnn_W_fuse', 'L1_gnn_b_fuse', 'L1_gnn_W_gate', 'L1_gnn_b_gate', 'L2_gnn_eps', 'L2_gnn_W1', 'L2_gnn_b1',
       'L2_gnn_gamma', 'L2_gnn_beta', 'L2_gnn_W2', 'L2_gnn_b2', 'L3_gnn_lambda_max', 'L3_gnn_W', 'L3_gnn_b']


def kernel(**inputs):
    import numpy as np
    import concourse.bacc as bacc
    from concourse import mybir as mb
    from concourse.bass_utils import run_bass_kernel_spmd

    nc = bacc.Bacc("TRN2", target_bir_lowering=False, num_devices=1)
    arrays, args = {}, {}
    for name in INS:
        v = np.ascontiguousarray(inputs[name])
        if v.ndim == 0:
            v = v.reshape(1)
        arrays[f"in_{name}"] = v
        args[name] = nc.dram_tensor(f"in_{name}", v.shape, mb.dt.from_np(v.dtype), kind="ExternalInput").ap()
    out = nc.dram_tensor("out", (N, D), F32, kind="ExternalOutput").ap()
    build(nc, args, out)
    r = run_bass_kernel_spmd(nc, [arrays], core_ids=[0])
    return r.results[0]["out"]
```
